# Optimizing a Trainium2 kernel written in Bass

```python
import numpy as np
import jax
import jax.numpy as jnp

def _softmax(x, axis=-1):
    return jax.nn.softmax(x, axis=axis)

def _gelu(x):
    return jax.nn.gelu(x, approximate=True)

def _silu(x):
    return jax.nn.silu(x)

def _sigmoid(x):
    return jax.nn.sigmoid(x)

def _layernorm(x, axis=-1, eps=1e-05):
    m = jnp.mean(x, axis=axis, keepdims=True)
    v = jnp.var(x, axis=axis, keepdims=True)
    return (x - m) / jnp.sqrt(v + eps)

def _scatter_add(tgt, idx, src, axis=0):
    return tgt.at[idx].add(src)

def _segment_sum(src, seg, n):
    return jax.ops.segment_sum(src, seg, n)
kernel_name = 'mk_cond_seq_d2_seqx_r2_f769ee'

def setup_inputs(seed: int=0):
    np.random.seed(seed)
    _w = jnp.asarray

    def _rec_inputs():
        import jax
        import jax.numpy as jnp
        _rk = jax.random.key(seed)
        x = 7.22e-05 + 1 * jax.random.normal(jax.random.fold_in(_rk, 1), (4, 1024, 512), jnp.float32)
        _lenS = 1024 - jax.random.randint(jax.random.fold_in(_rk, 7), (4,), 0, max(1, 1024 // 4) + 1, jnp.int32)
        _lenS2 = 1024 - jax.random.randint(jax.random.fold_in(_rk, 8), (4,), 0, max(1, 1024 // 4) + 1, jnp.int32)
        cond_1024 = 0.0061147 + 1.02565 * jax.random.normal(jax.random.fold_in(_rk, 11), (4, 512), jnp.float32)
        _validS = jnp.arange(1024)[None, :] < _lenS[:, None]
        _validS2 = jnp.arange(1024)[None, :] < _lenS2[:, None]
        _causal = jnp.tril(jnp.ones((1024, 1024), dtype=bool))
        mask_BxS_bk0 = jnp.logical_not(jnp.broadcast_to(_validS[:, :], (4, 1024)))
        return (x, cond_1024, mask_BxS_bk0)
    x, cond_1024, mask_BxS_bk0 = _rec_inputs()

    def _L0_cond_setup():
        import jax, jax.numpy as jnp
        import numpy as np
        D = 512
        H = 16
        HD = D // H
        MLP = 4 * D

        def _lin(key, fin, fout):
            k1, k2 = jax.random.split(key)
            lim = 1.0 / np.sqrt(fin)
            W = jax.random.uniform(k1, (fin, fout), minval=-lim, maxval=lim, dtype=jnp.float32)
            b = jax.random.uniform(k2, (fout,), minval=-lim, maxval=lim, dtype=jnp.float32)
            return (W, b)

        def layernorm(x, g, b, eps=1e-05):
            mu = jnp.mean(x, axis=-1, keepdims=True)
            var = jnp.var(x, axis=-1, keepdims=True)
            return (x - mu) * jax.lax.rsqrt(var + eps) * g + b

        def attention(h, Wqkv, bqkv, Wproj, bproj):
            B, L, _ = h.shape
            qkv = (h @ Wqkv + bqkv).reshape(B, L, 3, H, HD)
            q, k, v = jnp.moveaxis(qkv, 2, 0)
            scale = HD ** (-0.5)
            attn = jnp.einsum('blhd,bmhd->bhlm', q, k) * scale
            attn = jax.nn.softmax(attn, axis=-1)
            out = jnp.einsum('bhlm,bmhd->blhd', attn, v).reshape(B, L, D)
            return out @ Wproj + bproj
        key = jax.random.key(seed)
        ks = jax.random.split(key, 10)
        x = jax.random.normal(ks[0], (4, 1024, D), dtype=jnp.float32)
        time_emb = jax.random.normal(ks[1], (4, D), dtype=jnp.float32)
        Wqkv, bqkv = _lin(ks[2], D, 3 * D)
        Wproj, bproj = _lin(ks[3], D, D)
        W1, b1 = _lin(ks[4], D, MLP)
        W2, b2 = _lin(ks[5], MLP, D)
        Wt, bt = _lin(ks[6], D, 6 * D)
        g1 = jnp.ones((D,), jnp.float32)
        be1 = jnp.zeros((D,), jnp.float32)
        g2 = jnp.ones((D,), jnp.float32)
        be2 = jnp.zeros((D,), jnp.float32)
        return {'x': x, 'time_emb': time_emb, 'Wqkv': Wqkv, 'bqkv': bqkv, 'Wproj': Wproj, 'bproj': bproj, 'W1': W1, 'b1': b1, 'W2': W2, 'b2': b2, 'Wt': Wt, 'bt': bt, 'g1': g1, 'be1': be1, 'g2': g2, 'be2': be2}
    _L0_cond_all = _L0_cond_setup()
    _L0_cond_in = {k: v for k, v in _L0_cond_all.items() if k in ('Wqkv', 'bqkv', 'Wproj', 'bproj', 'W1', 'b1', 'W2', 'b2', 'Wt', 'bt', 'g1', 'be1', 'g2', 'be2')}
    del _L0_cond_all

    def _L1_cond_setup():
        import jax, jax.numpy as jnp
        import numpy as np
        B, L, D = (8, 1024, 512)
        FF_MULT = 2
        EPS = 1e-06

        def _layernorm(x):
            mu = jnp.mean(x, axis=-1, keepdims=True)
            var = jnp.mean(jnp.square(x - mu), axis=-1, keepdims=True)
            return (x - mu) / jnp.sqrt(var + EPS)

        def _ssm_fallback(u, w1, b1, w2, b2):
            h = jax.nn.gelu(u @ w1 + b1, approximate=False)
            return h @ w2 + b2
        key = jax.random.key(seed)
        ks = jax.random.split(key, 20)
        s = 0.02
        inp = {'x': jax.random.normal(ks[0], (B, L, D), jnp.float32), 't': jax.random.normal(ks[1], (B, D), jnp.float32), 'mask': jax.random.randint(ks[2], (B, L), 0, 2) > 0, 'ada_w': jax.random.normal(ks[3], (D, 3 * D), jnp.float32) * s, 'ada_b': jnp.zeros((3 * D,), jnp.float32), 'ssm_w1': jax.random.normal(ks[4], (D, D), jnp.float32) * s, 'ssm_b1': jnp.zeros((D,), jnp.float32), 'ssm_w2': jax.random.normal(ks[5], (D, D), jnp.float32) * s, 'ssm_b2': jnp.zeros((D,), jnp.float32), 'bwd_w1': jax.random.normal(ks[6], (D, D), jnp.float32) * s, 'bwd_b1': jnp.zeros((D,), jnp.float32), 'bwd_w2': jax.random.normal(ks[7], (D, D), jnp.float32) * s, 'bwd_b2': jnp.zeros((D,), jnp.float32), 'ffada_w': jax.random.normal(ks[8], (D, 3 * D), jnp.float32) * s, 'ffada_b': jnp.zeros((3 * D,), jnp.float32), 'ff_w1': jax.random.normal(ks[9], (D, FF_MULT * D), jnp.float32) * s, 'ff_b1': jnp.zeros((FF_MULT * D,), jnp.float32), 'ff_w2': jax.random.normal(ks[10], (FF_MULT * D, D), jnp.float32) * s, 'ff_b2': jnp.zeros((D,), jnp.float32)}
        return inp
    _L1_cond_all = _L1_cond_setup()
    _L1_cond_in = {k: v for k, v in _L1_cond_all.items() if k in ('ada_w', 'ada_b', 'ssm_w1', 'ssm_b1', 'ssm_w2', 'ssm_b2', 'bwd_w1', 'bwd_b1', 'bwd_w2', 'bwd_b2', 'ffada_w', 'ffada_b', 'ff_w1', 'ff_b1', 'ff_w2', 'ff_b2')}
    del _L1_cond_all
    return {'x': x, 'cond_1024': cond_1024, 'mask_BxS_bk0': mask_BxS_bk0, 'L0_cond_Wqkv': _L0_cond_in['Wqkv'], 'L0_cond_bqkv': _L0_cond_in['bqkv'], 'L0_cond_Wproj': _L0_cond_in['Wproj'], 'L0_cond_bproj': _L0_cond_in['bproj'], 'L0_cond_W1': _L0_cond_in['W1'], 'L0_cond_b1': _L0_cond_in['b1'], 'L0_cond_W2': _L0_cond_in['W2'], 'L0_cond_b2': _L0_cond_in['b2'], 'L0_cond_Wt': _L0_cond_in['Wt'], 'L0_cond_bt': _L0_cond_in['bt'], 'L0_cond_g1': _L0_cond_in['g1'], 'L0_cond_be1': _L0_cond_in['be1'], 'L0_cond_g2': _L0_cond_in['g2'], 'L0_cond_be2': _L0_cond_in['be2'], 'L1_cond_ada_w': _L1_cond_in['ada_w'], 'L1_cond_ada_b': _L1_cond_in['ada_b'], 'L1_cond_ssm_w1': _L1_cond_in['ssm_w1'], 'L1_cond_ssm_b1': _L1_cond_in['ssm_b1'], 'L1_cond_ssm_w2': _L1_cond_in['ssm_w2'], 'L1_cond_ssm_b2': _L1_cond_in['ssm_b2'], 'L1_cond_bwd_w1': _L1_cond_in['bwd_w1'], 'L1_cond_bwd_b1': _L1_cond_in['bwd_b1'], 'L1_cond_bwd_w2': _L1_cond_in['bwd_w2'], 'L1_cond_bwd_b2': _L1_cond_in['bwd_b2'], 'L1_cond_ffada_w': _L1_cond_in['ffada_w'], 'L1_cond_ffada_b': _L1_cond_in['ffada_b'], 'L1_cond_ff_w1': _L1_cond_in['ff_w1'], 'L1_cond_ff_b1': _L1_cond_in['ff_b1'], 'L1_cond_ff_w2': _L1_cond_in['ff_w2'], 'L1_cond_ff_b2': _L1_cond_in['ff_b2']}

def reference(x, cond_1024, mask_BxS_bk0, L0_cond_Wqkv, L0_cond_bqkv, L0_cond_Wproj, L0_cond_bproj, L0_cond_W1, L0_cond_b1, L0_cond_W2, L0_cond_b2, L0_cond_Wt, L0_cond_bt, L0_cond_g1, L0_cond_be1, L0_cond_g2, L0_cond_be2, L1_cond_ada_w, L1_cond_ada_b, L1_cond_ssm_w1, L1_cond_ssm_b1, L1_cond_ssm_w2, L1_cond_ssm_b2, L1_cond_bwd_w1, L1_cond_bwd_b1, L1_cond_bwd_w2, L1_cond_bwd_b2, L1_cond_ffada_w, L1_cond_ffada_b, L1_cond_ff_w1, L1_cond_ff_b1, L1_cond_ff_w2, L1_cond_ff_b2):
    import jax
    import jax.numpy as jnp

    def _L0_cond_ref(x, time_emb, Wqkv, bqkv, Wproj, bproj, W1, b1, W2, b2, Wt, bt, g1, be1, g2, be2):
        import jax, jax.numpy as jnp
        import numpy as np
        D = 512
        H = 16
        HD = D // H
        MLP = 4 * D

        def _lin(key, fin, fout):
            k1, k2 = jax.random.split(key)
            lim = 1.0 / np.sqrt(fin)
            W = jax.random.uniform(k1, (fin, fout), minval=-lim, maxval=lim, dtype=jnp.float32)
            b = jax.random.uniform(k2, (fout,), minval=-lim, maxval=lim, dtype=jnp.float32)
            return (W, b)

        def layernorm(x, g, b, eps=1e-05):
            mu = jnp.mean(x, axis=-1, keepdims=True)
            var = jnp.var(x, axis=-1, keepdims=True)
            return (x - mu) * jax.lax.rsqrt(var + eps) * g + b

        def attention(h, Wqkv, bqkv, Wproj, bproj):
            B, L, _ = h.shape
            qkv = (h @ Wqkv + bqkv).reshape(B, L, 3, H, HD)
            q, k, v = jnp.moveaxis(qkv, 2, 0)
            scale = HD ** (-0.5)
            attn = jnp.einsum('blhd,bmhd->bhlm', q, k) * scale
            attn = jax.nn.softmax(attn, axis=-1)
            out = jnp.einsum('bhlm,bmhd->blhd', attn, v).reshape(B, L, D)
            return out @ Wproj + bproj
        tp = (jax.nn.silu(time_emb) @ Wt + bt)[:, None, :]
        shift_msa, scale_msa, gate_msa, shift_mlp, scale_mlp, gate_mlp = jnp.split(tp, 6, axis=-1)
        h = layernorm(x, g1, be1)
        h = h * (1.0 + scale_msa) + shift_msa
        h = attention(h, Wqkv, bqkv, Wproj, bproj)
        x = x + gate_msa * h
        h = layernorm(x, g2, be2)
        h = h * (1.0 + scale_mlp) + shift_mlp
        h = jax.nn.gelu(h @ W1 + b1, approximate=False) @ W2 + b2
        x = x + gate_mlp * h
        return x

    def _L1_cond_ref(x, t, mask, ada_w, ada_b, ssm_w1, ssm_b1, ssm_w2, ssm_b2, bwd_w1, bwd_b1, bwd_w2, bwd_b2, ffada_w, ffada_b, ff_w1, ff_b1, ff_w2, ff_b2):
        import jax, jax.numpy as jnp
        import numpy as np
        B, L, D = (8, 1024, 512)
        FF_MULT = 2
        EPS = 1e-06

        def _layernorm(x):
            mu = jnp.mean(x, axis=-1, keepdims=True)
            var = jnp.mean(jnp.square(x - mu), axis=-1, keepdims=True)
            return (x - mu) / jnp.sqrt(var + EPS)

        def _ssm_fallback(u, w1, b1, w2, b2):
            h = jax.nn.gelu(u @ w1 + b1, approximate=False)
            return h @ w2 + b2
        m = mask[:, :, None]
        emb = jax.nn.silu(t) @ ada_w + ada_b
        shift, scale, gate_msa = jnp.split(emb, 3, axis=1)
        norm = _layernorm(x) * (1.0 + scale[:, None]) + shift[:, None]
        norm = jnp.where(m, norm, 0.0)
        fwd = _ssm_fallback(norm, ssm_w1, ssm_b1, ssm_w2, ssm_b2)
        bwd = jnp.flip(_ssm_fallback(jnp.flip(norm, axis=1), bwd_w1, bwd_b1, bwd_w2, bwd_b2), axis=1)
        ssm_out = jnp.where(m, fwd + bwd, 0.0)
        x = x + gate_msa[:, None] * ssm_out
        ff_ada = jax.nn.silu(t) @ ffada_w + ffada_b
        shift_mlp, scale_mlp, gate_mlp = jnp.split(ff_ada, 3, axis=1)
        ff_norm = _layernorm(x) * (1.0 + scale_mlp[:, None]) + shift_mlp[:, None]
        h = jax.nn.gelu(ff_norm @ ff_w1 + ff_b1, approximate=True)
        ff_out = h @ ff_w2 + ff_b2
        return x + gate_mlp[:, None] * ff_out
    x = _L0_cond_ref(x, cond_1024, L0_cond_Wqkv, L0_cond_bqkv, L0_cond_Wproj, L0_cond_bproj, L0_cond_W1, L0_cond_b1, L0_cond_W2, L0_cond_b2, L0_cond_Wt, L0_cond_bt, L0_cond_g1, L0_cond_be1, L0_cond_g2, L0_cond_be2)
    x = _L1_cond_ref(x, cond_1024, mask_BxS_bk0, L1_cond_ada_w, L1_cond_ada_b, L1_cond_ssm_w1, L1_cond_ssm_b1, L1_cond_ssm_w2, L1_cond_ssm_b2, L1_cond_bwd_w1, L1_cond_bwd_b1, L1_cond_bwd_w2, L1_cond_bwd_b2, L1_cond_ffada_w, L1_cond_ffada_b, L1_cond_ff_w1, L1_cond_ff_b1, L1_cond_ff_w2, L1_cond_ff_b2)
    return x

_drawn_inputs = setup_inputs


def setup_inputs(seed=0):
    import zlib

    import numpy as np

    out = dict(_drawn_inputs(seed))
    spreads = {'L0_cond_g1': (1.0, 0.6),
     'L0_cond_be1': (0.0, 0.562),
     'L0_cond_g2': (1.0, 0.6),
     'L0_cond_be2': (0.0, 0.8),
     'L1_cond_ada_b': (0.0, 0.8),
     'L1_cond_ssm_b1': (0.0, 0.8),
     'L1_cond_ssm_b2': (0.0, 0.8),
     'L1_cond_bwd_b1': (0.0, 0.8),
     'L1_cond_bwd_b2': (0.0, 0.8),
     'L1_cond_ffada_b': (0.0, 0.359),
     'L1_cond_ff_b1': (0.0, 0.716),
     'L1_cond_ff_b2': (0.0, 0.386)}
    factors = {'L0_cond_bqkv': 8.0,
     'L0_cond_bproj': 6.065,
     'L0_cond_b1': 8.0,
     'L0_cond_b2': 8.0,
     'L0_cond_bt': 6.996,
     'L1_cond_ssm_w1': 4.75,
     'L1_cond_ssm_w2': 4.484,
     'L1_cond_bwd_w1': 4.709,
     'L1_cond_bwd_w2': 4.382}
    for name, (base, spread) in spreads.items():
        noise = np.random.default_rng([zlib.crc32(name.encode()), seed]).standard_normal(out[name].shape)
        drawn = base * np.exp(spread * noise) if base else spread * noise
        out[name] = jnp.asarray(drawn.astype(out[name].dtype))
    for name, factor in factors.items():
        out[name] = (out[name] * factor).astype(out[name].dtype)
    return out
```

```python
from contextlib import ExitStack

import numpy as np

import concourse.bass as bass
from concourse import mybir

F32 = mybir.dt.float32
F16 = mybir.dt.float16
BF16 = mybir.dt.bfloat16
U8 = mybir.dt.uint8
ALU = mybir.AluOpType
ACT = mybir.ActivationFunctionType
AX_X = mybir.AxisListType.X

P = 128
NB = 4
L = 1024
D = 512
H = 16
HD = D // H
KC = D // P
TILE = 512
TG = TILE // P
NT = L // TILE
GPB = L // P
SCALE = float(HD) ** -0.5
M_UNIT = 64.0
VW = 2 * HD + 1
VP = VW + 1
STACK = 3 * HD

U_QKV, U_PROJ = 0, 3
N_ATT_UNITS = 4
N_FF_UNITS = 16
SITES = [
    dict(chunks=16, up=0, down=4, eps=1e-5, bias=0, act=ACT.Gelu),
    dict(chunks=8, up=8, down=10, eps=1e-6, bias=16, act=ACT.Gelu),
    dict(chunks=8, up=12, down=14, eps=1e-6, bias=24, act=ACT.Gelu_apprx_tanh),
]
C_ADA = 0
C_G1, C_BE1, C_G2, C_BE2 = 32, 36, 40, 44
C_QK = 48
C_UP = 56
NCOLS = 88
R_GATE, R_OUT, R_BWD, R_V = 0, 4, 8, 9
NROWS = 10

NST = 3
RING = 4
LAG = 3
DVE_PAIRS = (3, 7)
SM_AT = ((0, 1), (2,), (3, 4), (5,), (6,), (7,), (), ())
POOL_PAIRS = tuple(r for r in range(8) if r not in DVE_PAIRS)


def prologue(nc, ctx, t, dram):
    def sb(name, shape, dt):
        return ctx.enter_context(nc.sbuf_tensor(name, shape, dt))

    def sem(name):
        return ctx.enter_context(nc.semaphore(name))

    NSTG = 3
    stage = [sb(f"stage{i}", [P, KC, D], F32) for i in range(NSTG)]
    condT = sb("condT", [P, KC, NB], F32)
    sil = sb("sil", [P, KC, NB], F32)
    vec = sb("vec", [P, 4, 2, KC, NB], F32)
    one_plus = sb("one_plus", [P, 4, KC, NB], F32)
    rows4 = sb("rows4", [NB, NROWS, D], F32)
    gates = sb("gates", [NB, 4, 2, D], F32)
    mask_u8 = sb("mask_u8", [P, NB * GPB], U8)
    p_vec = [ctx.enter_context(nc.psum_tensor(f"p_vec{i}", [P, D], F32)) for i in range(4)]
    pv = [p[:, 0:2 * KC * NB].rearrange("p (k m b) -> p k m b", k=2, m=KC) for p in p_vec]
    pg = [ctx.enter_context(nc.psum_tensor(f"p_gate{i}", [P, D], F32)) for i in range(2)]

    small_in = sem("small_in")
    stage_in = [sem(f"stage_in{i}") for i in range(NSTG)]
    sil_done = sem("sil_done")
    unit_used = sem("unit_used")
    vec_step = sem("vec_step")
    gate_read = sem("gate_read")
    gates_out = sem("gates_out")
    hi_done = sem("hi_done")
    lo_done = sem("lo_done")
    N_ADA = 12

    with nc.Block() as block:

        @block.sync
        def _(sp):
            sp.dma_start(condT[:], dram["condT"]).then_inc(small_in, 16)
            sp.dma_start(t["cols"][:], dram["cols"]).then_inc(small_in, 16)
            sp.dma_start(t["ident"][:], dram["ident"]).then_inc(small_in, 16)
            sp.dma_start(mask_u8[:], dram["mask"]).then_inc(small_in, 16)
            sp.dma_start(rows4[:].rearrange("b r n -> b (r n)"),
                         dram["rows"].rearrange("r n -> (r n)").partition_broadcast(NB)).then_inc(small_in, 16)
            sp.dma_start(t["bv"][:], dram["rows"][R_V].partition_broadcast(P)).then_inc(small_in, 16)
            for n in range(N_ADA + N_ATT_UNITS):
                if n >= NSTG:
                    old = n - NSTG
                    if old < N_ADA:
                        sp.wait_ge(unit_used, old + 1)
                    else:
                        sp.wait_ge(lo_done, old - N_ADA + 1)
                src = dram["ada"][n] if n < N_ADA else dram["w"][n - N_ADA]
                sp.dma_start(stage[n % NSTG][:].rearrange("p k n -> p (k n)"), src).then_inc(stage_in[n % NSTG], 16)
            sp.wait_ge(gate_read, 4)
            for s in range(4):
                sp.dma_start(dram["gates"][s, 0:NB], gates[:, s]).then_inc(gates_out, 16)
                sp.dma_start(dram["gates"][s, NB:NB + 1], gates[0:1, s]).then_inc(gates_out, 16)
            sp.wait_ge(gates_out, 8 * 16)

        @block.scalar
        def _(act):
            act.wait_ge(small_in, 96)
            nc.scalar.activation(sil[:], condT[:], ACT.Silu).then_inc(sil_done, 1)
            for u in range(N_ATT_UNITS):
                n = N_ADA + u
                act.wait_ge(stage_in[n % NSTG], 16 * (n // NSTG + 1))
                nc.scalar.copy(t["wa_hi"][:, u], stage[n % NSTG][:]).then_inc(hi_done, 1)

        @block.tensor
        def _(pe):
            pe.wait_ge(sil_done, 1)
            for n in range(N_ADA):
                site, part = divmod(n, 3)
                w = stage[n % NSTG]
                pe.wait_ge(stage_in[n % NSTG], 16 * (n // NSTG + 1))
                if part < 2:
                    for m in range(KC):
                        for kc in range(KC):
                            mm = nc.tensor.matmul(pv[site][:, part, m, :], w[:, kc, m * P:(m + 1) * P], sil[:, kc, :],
                                                  start=(kc == 0), stop=(kc == KC - 1))
                else:
                    if site >= 2:
                        pe.wait_ge(gate_read, site - 1)
                    for kc in range(KC):
                        mm = nc.tensor.matmul(pg[site % 2][0:NB, :], sil[:, kc, :], w[:, kc, :],
                                              start=(kc == 0), stop=(kc == KC - 1))
                mm.then_inc(unit_used, 1)

        @block.vector
        def _(dve):
            step = 0

            def then(ins):
                nonlocal step
                step += 1
                ins.then_inc(vec_step, 1)
                dve.wait_ge(vec_step, step)

            cols = t["cols"]
            dve.wait_ge(small_in, 96)
            nc.vector.tensor_copy(t["ident16"][:], t["ident"][:])
            nc.vector.tensor_copy(t["mask"][:], mask_u8[:])
            then(nc.vector.tensor_tensor(rows4[:, R_OUT + 2, :], rows4[:, R_OUT + 2, :], rows4[:, R_BWD, :], ALU.add))
            for a in (t["ln_a"], t["ln_b"]):
                then(nc.vector.memset(a[:], 1.0))
            for site in range(4):
                dve.wait_ge(unit_used, 3 * site + 3)
                then(nc.vector.tensor_tensor(
                    vec[:, site], pv[site],
                    cols[:, C_ADA + 8 * site:C_ADA + 8 * site + 8].rearrange("p (k m) -> p k m", k=2)
                    .unsqueeze(3).to_broadcast([P, 2, KC, NB]), ALU.add))
                a, b = t["ln_a"][:, site, :, 0:NB], t["ln_b"][:, site, :, 0:NB]
                if site < 2:
                    g = cols[:, (C_G1, C_G2)[site]:(C_G1, C_G2)[site] + KC].unsqueeze(2).to_broadcast([P, KC, NB])
                    be = cols[:, (C_BE1, C_BE2)[site]:(C_BE1, C_BE2)[site] + KC].unsqueeze(2).to_broadcast([P, KC, NB])
                    then(nc.vector.tensor_scalar(one_plus[:, site], vec[:, site, 1], 1.0, None, ALU.add))
                    then(nc.vector.tensor_tensor(a, one_plus[:, site], g, ALU.mult))
                    then(nc.vector.tensor_tensor(b, one_plus[:, site], be, ALU.mult))
                    then(nc.vector.tensor_tensor(b, b, vec[:, site, 0], ALU.add))
                else:
                    then(nc.vector.tensor_scalar(a, vec[:, site, 1], 1.0, None, ALU.add))
                    then(nc.vector.tensor_copy(b, vec[:, site, 0]))
                then(nc.vector.tensor_tensor(gates[:, site, 0, :], pg[site % 2][0:NB, :], rows4[:, R_GATE + site, :], ALU.add))
                nc.vector.tensor_tensor(gates[:, site, 1, :], gates[:, site, 0, :], rows4[:, R_OUT + site, :],
                                        ALU.mult).then_inc(gate_read, 1)
            for u in range(N_ATT_UNITS):
                dve.wait_ge(hi_done, u + 1)
                nc.vector.tensor_tensor(t["wa_lo"][:, u], stage[(N_ADA + u) % NSTG][:], t["wa_hi"][:, u],
                                        ALU.subtract).then_inc(lo_done, 1)


def attention(nc, ctx, t, dram):
    def sb(name, shape, dt):
        return ctx.enter_context(nc.sbuf_tensor(name, shape, dt))

    def sem(name):
        return ctx.enter_context(nc.semaphore(name))

    xt = [sb(f"xt{u}", [P, TG, D], F32) for u in range(NT)]
    stats = sb("stats", [P, NT, TG, 6], F32)
    mv = sb("mv", [P, NT, TG, 2], F32)
    var_eps = sb("var_eps", [P, NT, TG], F32)
    rstd = sb("rstd", [P, NT, TG], F32)
    h_hi = sb("h_hi", [P, KC, TILE], F16)
    h_lo = sb("h_lo", [P, KC, TILE], BF16)
    r32 = [sb(f"r32_{i}", [P, TILE], F32) for i in range(4)]
    qk_hi = sb("qk_hi", [P, 2 * KC, L], F16)
    qk_lo = sb("qk_lo", [P, 2 * KC, L], F16)
    v32 = [sb(f"v32_{i}", [P, D], F32) for i in range(2)]
    v_all = sb("v_all", [P, H, GPB, VP], F16)
    q_st = [sb(f"q_st{e}", [P, L], F16) for e in range(NST)]
    k_st = [sb(f"k_st{e}", [P, L], F16) for e in range(NST)]
    p32 = [sb(f"p32_{i}", [P, 2, TILE], F32) for i in range(RING)]
    p_lo = [sb(f"p_lo{i}", [P, 2, TILE], F16) for i in range(RING)]
    row_max = sb("row_max", [P, 2, GPB], F32)
    neg_max = sb("neg_max", [P, 2, GPB], F16)
    o_tmp = [sb(f"o_tmp{i}", [P, TG, HD], F32) for i in range(2)]
    o_sum = [sb(f"o_sum{i}", [P, TG, HD], F32) for i in range(2)]
    inv_l = [sb(f"inv_l{i}", [P, TG], F32) for i in range(2)]
    o_rows = sb("o_rows", [P, GPB, D], F32)
    gate = sb("gate_att", [P, 2, D], F32)
    gated = [sb(f"gated{i}", [P, D], F32) for i in range(2)]
    waited = sb("waited", [P, 1], F32)
    ln_ab = sb("ln_ab_att", [P, 2, KC], F32)

    s_max = [ctx.enter_context(nc.psum_tensor(f"s_max{i}", [P, L], F32)) for i in range(2)]
    s_exp = [ctx.enter_context(nc.psum_tensor(f"s_exp{i}", [P, TILE], F32)) for i in range(2)]
    pv = [ctx.enter_context(nc.psum_tensor(f"pv{i}", [P, TG, P], F32)) for i in range(2)]

    def work(i):
        return s_max[i // 2][:, i % 2 * TILE:i % 2 * TILE + TILE]

    x_in = [sem(f"x_in{u}") for u in range(NT)]
    bn_done = sem("bn_done")
    agg_done = sem("agg_done")
    var_done = sem("var_done")
    rstd_done = sem("rstd_done")
    x_ready = sem("x_ready")
    tp_full = sem("tp_full")
    wk_full = sem("wk_full")
    r32_full = sem("r32_full")
    split_hi = sem("split_hi")
    split_done = sem("split_done")
    v_add = sem("v_add")
    stack_in = [sem(f"stack_in{e}") for e in range(NST)]
    sm_full = sem("sm_full")
    sm_free = sem("sm_free")
    max_done = sem("max_done")
    mrow_full = sem("mrow_full")
    mrow_done = sem("mrow_done")
    st_full = sem("st_full")
    exp_done = sem("exp_done")
    lo_pool = sem("lo_pool")
    lo_dve = sem("lo_dve")
    pv_done = sem("pv_done")
    o_tmp_done = sem("o_tmp_done")
    inv_done = sem("inv_done")
    norm_done = sem("norm_done")
    o_ready = sem("o_ready")
    gate_in = sem("gate_in")
    x_biased = sem("x_biased")
    gated_done = sem("gated_done")
    x1_ready = sem("x1_ready")
    x1_out = [sem(f"x1_out{u}") for u in range(NT)]
    ab_ready = sem("ab_ready")
    sp_turn = sem("sp_turn")
    consts = sem("consts")

    NPL, NDV = len(POOL_PAIRS), len(DVE_PAIRS)
    HEAD_DMAS = 6

    with nc.Block() as block:

        @block.sync
        def _(sp):
            def wait(sem_, value):
                sp.wait_ge(sem_, sp.snap(value))
                sp.sem_inc(sp_turn, 1)

            sp.wait_ge(consts, 1)

            with sp.Fori(0, NB) as b:
                for u in range(NT):
                    sp.dma_start(xt[u][:], dram["x"][bass.ds(b * NT + u, 1)].rearrange("t p g n -> p (t g) n")).then_inc(x_in[u], 16)
                sp.dma_start(gate[:], dram["gates"][0, bass.ds(b, 1)].rearrange("b k n -> (b k n)").partition_broadcast(P)).then_inc(gate_in, 16)
                wait(split_done, b * 40 + 32)
                for h in range(H):
                    g, j, e = h // 4, h % 4, h % NST
                    if h >= NST:
                        wait(st_full, b * (16 * H) + 16 * (h - NST + 1))
                    part = slice(j * HD, (j + 1) * HD)
                    for dst, at, src, chunk in ((q_st, 0, qk_hi, g), (q_st, 1, qk_lo, g), (q_st, 2, qk_hi, g),
                                                (k_st, 0, qk_hi, KC + g), (k_st, 1, qk_hi, KC + g),
                                                (k_st, 2, qk_lo, KC + g)):
                        sp.dma_start(dst[e][at * HD:(at + 1) * HD, :], src[part, chunk, :]).then_inc(stack_in[e], 16)
                for u in range(NT):
                    sp.dma_start(xt[u][:], dram["x"][bass.ds(b * NT + u, 1)].rearrange("t p g n -> p (t g) n")).then_inc(x_in[u], 16)
                for u in range(NT):
                    wait(x1_ready, b * 8 + 4 * (u + 1))
                    sp.dma_start(dram["x1"][bass.ds(b * NT + u, 1)].rearrange("t p g n -> p (t g) n"), xt[u][:]).then_inc(x1_out[u], 16)
                for u in range(NT):
                    wait(x1_out[u], b * 16 + 16)

        @block.tensor
        def _(pe):
            wa = (t["wa_hi"], t["wa_lo"])
            hh = (h_hi, h_lo)

            def transposes(rows, wait_bank):
                for fc in range(KC):
                    wait_bank(fc)
                    for g in range(TG):
                        mm = nc.tensor.transpose(s_exp[fc % 2][:, g * P:(g + 1) * P], rows(g)[:, fc * P:(fc + 1) * P],
                                                 t["ident"][:])
                    mm.then_inc(tp_full, 1)

            def product(out, lhs, rhs):
                for kc in range(KC):
                    for k, (a, c) in enumerate(((0, 0), (0, 1), (1, 0))):
                        mm = nc.tensor.matmul(out, lhs(a, kc), rhs(c, kc), start=(kc == 0 and k == 0),
                                              stop=(kc == KC - 1 and k == 2))
                mm.then_inc(wk_full, 1)

            def scores_for_max(b, h, i):
                e = h % 2
                q, k = q_st[h % NST], k_st[h % NST]
                if i == 0:
                    slot_heads = len(range(h % NST, H, NST))
                    pe.wait_ge(stack_in[h % NST], b * (16 * HEAD_DMAS * slot_heads) + 16 * HEAD_DMAS * (h // NST + 1))
                if i == 1:
                    pe.wait_ge(mrow_done, b * H + h + 1)
                else:
                    pe.wait_ge(sm_free, b * (8 * H) + 8 * h + max(i, 1))
                for j in range(2):
                    mm = nc.tensor.matmul(s_max[(e + i) % 2][:, j * TILE:(j + 1) * TILE], q[0:STACK, i * P:(i + 1) * P],
                                          k[0:STACK, j * TILE:(j + 1) * TILE], start=True, stop=True)
                mm.then_inc(sm_full, 1)

            def row_of_maxima(b, h):
                e = h % 2
                pe.wait_ge(max_done, b * H + h + 1)
                for i in range(GPB):
                    mm = nc.tensor.matmul(s_max[e][STACK:STACK + 1, i * P:(i + 1) * P], neg_max[:, e, i:i + 1],
                                          t["ident16"][:], start=True, stop=True)
                mm.then_inc(mrow_full, 1)

            def scores_for_exp(b, h, i):
                half, kc = i // 8, i % 8
                if i == 0:
                    pe.wait_ge(mrow_done, b * H + h + 2)
                pe.wait_ge(exp_done, b * (16 * H) + 16 * h + i + 1)
                nc.tensor.matmul(s_exp[i % 2][:], k_st[h % NST][0:STACK + 1, kc * P:(kc + 1) * P],
                                 q_st[h % NST][0:STACK + 1, half * TILE:(half + 1) * TILE],
                                 start=True, stop=True).then_inc(st_full, 1)

            def use_pair(b, h, r):
                half = r // 4
                if r in DVE_PAIRS:
                    pe.wait_ge(lo_dve, b * (NDV * H) + NDV * h + DVE_PAIRS.index(r) + 1)
                else:
                    pe.wait_ge(lo_pool, b * (NPL * H) + NPL * h + POOL_PAIRS.index(r) + 1)
                if r % 4 == 0:
                    pe.wait_ge(norm_done, b * (2 * H) + 2 * h + half + 1)
                hi = p32[r % RING][:].rearrange("p c n -> p (c n)").bitcast(BF16)
                for c in range(2):
                    kc = r % 4 * 2 + c
                    for g in range(TG):
                        at = c * TILE + g * P
                        nc.tensor.matmul(pv[half][:, g, 0:VW], hi[:, 2 * at + 1:2 * (at + P):2], v_all[:, h, kc, 0:VW],
                                         start=(r % 4 == 0 and c == 0 and g == 0), stop=False, skip_group_check=True)
                        mm = nc.tensor.matmul(pv[half][:, g, HD:VW], p_lo[r % RING][:, c, g * P:(g + 1) * P],
                                              v_all[:, h, kc, HD:VW], start=False,
                                              stop=(r % 4 == 3 and c == 1), skip_group_check=True)
                mm.then_inc(pv_done, 1)

            pe.wait_ge(consts, 2)
            with pe.Fori(0, NB) as b:
                for u in range(NT):
                    pe.wait_ge(x_ready, b * 8 + 4 * (u + 1))
                    transposes(lambda g: xt[u][:, g, :],
                               lambda fc: pe.wait_ge(r32_full, b * 32 + 12 * u + fc - 1) if fc >= 2 else None)
                    pe.wait_ge(split_done, b * 40 + 16 * u + 4)
                    for c in range(2 * KC):
                        if c >= 4:
                            pe.wait_ge(r32_full, b * 32 + 12 * u + 4 + c - 3)
                        elif u == 1:
                            pe.wait_ge(v_add, b * 8 + c + 1)
                        elif c == 0:
                            pe.wait_ge(gated_done, b * 8 + 1)
                        product(work(c % 4),
                                lambda a, kc: wa[a][:, U_QKV + c // KC, kc, c % KC * P:(c % KC + 1) * P],
                                lambda a, kc: hh[a][:, kc, :])
                    for g in range(TG):
                        pe.wait_ge(r32_full, b * 32 + 12 * u + 8 + g + 1)
                        product(work(g), lambda a, kc: hh[a][:, kc, g * P:(g + 1) * P],
                                lambda a, kc: wa[a][:, U_QKV + 2, kc, :])
                pe.wait_ge(split_done, b * 40 + 32)
                for i in range(GPB):
                    scores_for_max(b, 0, i)
                row_of_maxima(b, 0)
                for h in range(H):
                    for r in range(8):
                        if h + 1 < H:
                            for i in SM_AT[r]:
                                scores_for_max(b, h + 1, i)
                            if r == 7:
                                row_of_maxima(b, h + 1)
                        scores_for_exp(b, h, 2 * r)
                        scores_for_exp(b, h, 2 * r + 1)
                        if r >= LAG:
                            use_pair(b, h, r - LAG)
                        elif h:
                            use_pair(b, h - 1, r - LAG + 8)
                for r in range(8 - LAG, 8):
                    use_pair(b, H - 1, r)
                for u in range(NT):
                    pe.wait_ge(o_ready, b * (2 * H) + 2 * H - 1 + u)
                    transposes(lambda g: o_rows[:, TG * u + g, :],
                               lambda fc: pe.wait_ge(r32_full, b * 32 + 24 + 4 * u + fc - 1) if fc >= 2 else None)
                    pe.wait_ge(split_done, b * 40 + 32 + 4 * u + 4)
                    for g in range(TG):
                        if u == 1:
                            pe.wait_ge(gated_done, b * 8 + g + 2)
                        product(work(g), lambda a, kc: hh[a][:, kc, g * P:(g + 1) * P],
                                lambda a, kc: wa[a][:, U_PROJ, kc, :])

        @block.scalar
        def _(act):
            def chunk32(n, src, func_args):
                nc.scalar.activation(r32[n % 4][:], src, ACT.Identity, **func_args).then_inc(r32_full, 1)

            def low_columns(b, h, half):
                act.wait_ge(pv_done, b * (8 * H) + 8 * h + 4 * (half + 1) + RING)
                nc.scalar.copy(o_tmp[half][:], pv[half][:, :, 0:HD]).then_inc(o_tmp_done, 1)

            def take_row(b, h):
                e = h % 2
                act.wait_ge(mrow_full, b * H + h + 1)
                nc.scalar.copy(q_st[h % NST][STACK:STACK + 1, :], s_max[e][STACK:STACK + 1, :]).then_inc(mrow_done, 1)

            act.wait_ge(consts, 2)
            with act.Fori(0, NB) as b:
                for k, ab in enumerate((t["ln_a"], t["ln_b"])):
                    nc.scalar.copy(ln_ab[:, k, :], ab[:, 0, :, bass.ds(b, 1)]).then_inc(ab_ready, 1)
                act.wait_ge(ab_ready, b * 2 + 2)
                for u in range(NT):
                    for fc in range(KC):
                        act.wait_ge(tp_full, b * 16 + 4 * u + fc + 1)
                        if u == 1:
                            act.wait_ge(split_done, b * 40 + 8 + fc + 1)
                        chunk32(fc, s_exp[fc % 2][:], dict(scale=ln_ab[:, 0, fc:fc + 1], bias=ln_ab[:, 1, fc:fc + 1]))
                    for c in range(2 * KC):
                        act.wait_ge(wk_full, b * 32 + 12 * u + c + 1)
                        act.wait_ge(split_done, b * 40 + 16 * u + c + 1)
                        chunk32(c, work(c % 4), dict(bias=t["cols"][:, C_QK + c:C_QK + c + 1]))
                take_row(b, 0)
                for h in range(H):
                    for r in range(8):
                        if r == 7 and h + 1 < H:
                            take_row(b, h + 1)
                        for i in (2 * r, 2 * r + 1):
                            act.wait_ge(st_full, b * (16 * H) + 16 * h + i + 1)
                            if i % 2 == 0:
                                act.wait_ge(pv_done, b * (8 * H) + 8 * h + r + 1)
                            nc.scalar.activation(p32[r % RING][:, i % 2, :], s_exp[i % 2][:], ACT.Exp,
                                                 scale=SCALE).then_inc(exp_done, 1)
                        if r == 3 and h:
                            low_columns(b, h - 1, 1)
                        if r == 7:
                            low_columns(b, h, 0)
                low_columns(b, H - 1, 1)
                for u in range(NT):
                    for fc in range(KC):
                        act.wait_ge(tp_full, b * 16 + 8 + 4 * u + fc + 1)
                        if u == 1:
                            act.wait_ge(split_done, b * 40 + 32 + fc + 1)
                        chunk32(fc, s_exp[fc % 2][:], {})

        @block.gpsimd
        def _(pool):
            minus_half = t["minus_half"]
            pool.wait_ge(consts, 2)
            with pool.Fori(0, NB) as b:
                for u in range(NT):
                    pool.wait_ge(var_done, b * NT + u + 1)
                    nc.gpsimd.tensor_tensor(rstd[:, u, :], var_eps[:, u, :], minus_half[:], ALU.pow).then_inc(rstd_done, 1)
                for h in range(H):
                    for r in POOL_PAIRS:
                        pool.wait_ge(exp_done, b * (16 * H) + 16 * h + 2 * r + 4)
                        hi = p32[r % RING][:].rearrange("p c n -> p (c n)").bitcast(BF16)[:, 1::2]
                        nc.gpsimd.tensor_tensor(p_lo[r % RING][:].rearrange("p c n -> p (c n)"),
                                                p32[r % RING][:].rearrange("p c n -> p (c n)"), hi,
                                                ALU.subtract).then_inc(lo_pool, 1)
                pool.wait_ge(gate_in, b * 16 + 16)
                for u in range(NT):
                    pool.wait_ge(x_in[u], b * 32 + 32)
                    for g in range(TG):
                        nc.gpsimd.tensor_tensor(xt[u][:, g, :], xt[u][:, g, :], gate[:, 1, :],
                                                ALU.add).then_inc(x_biased, 1)

        @block.vector
        def _(dve):
            def split(b, n, src, hi, lo):
                nc.vector.tensor_copy(hi, src).then_inc(split_hi, 1)
                dve.wait_ge(split_hi, b * 40 + n + 1)
                nc.vector.tensor_tensor(lo, src, hi, ALU.subtract).then_inc(split_done, 1)

            def take_max(b, h, i):
                e = h % 2
                dve.wait_ge(sm_full, b * (8 * H) + 8 * h + i + 1)
                nc.vector.reduce_max(row_max[:, e, i:i + 1], s_max[(e + i) % 2][:], AX_X).then_inc(sm_free, 1)

            def negate_max(b, h):
                e = h % 2
                dve.wait_ge(sm_free, b * (8 * H) + 8 * h + 8 + 1)
                nc.vector.tensor_scalar(neg_max[:, e, :], row_max[:, e, :], -1.0 / M_UNIT, None,
                                        ALU.mult).then_inc(max_done, 1)

            def low_part(b, h, r):
                dve.wait_ge(exp_done, b * (16 * H) + 16 * h + 2 * r + 4)
                flat = p32[r % RING][:].rearrange("p c n -> p (c n)")
                nc.vector.tensor_tensor(p_lo[r % RING][:].rearrange("p c n -> p (c n)"), flat,
                                        flat.bitcast(BF16)[:, 1::2], ALU.subtract).then_inc(lo_dve, 1)

            def normalise(b, h, half):
                n = 2 * h + half
                dve.wait_ge(o_tmp_done, b * (2 * H) + n + 1)
                nc.vector.reciprocal(inv_l[half][:], pv[half][:, :, VW - 1]).then_inc(inv_done, 1)
                nc.vector.tensor_tensor(o_sum[half][:], pv[half][:, :, HD:2 * HD], o_tmp[half][:],
                                        ALU.add).then_inc(norm_done, 1)
                dve.wait_ge(inv_done, b * (2 * H) + n + 1)
                dve.wait_ge(norm_done, b * (2 * H) + n + 3)
                nc.vector.tensor_tensor(o_rows[:, TG * half:TG * (half + 1), h * HD:(h + 1) * HD], o_sum[half][:],
                                        inv_l[half][:].unsqueeze(2).to_broadcast([P, TG, HD]),
                                        ALU.mult).then_inc(o_ready, 1)

            for e in range(NST):
                nc.vector.memset(k_st[e][STACK:STACK + 1, :], M_UNIT)
            for i in range(2):
                nc.vector.memset(inv_l[0][:, i:i + 1], 0.0).then_inc(exp_done, 1)
            for i in range(2):
                nc.vector.memset(t["minus_half"][:, 2 * i:2 * i + 2], -0.5).then_inc(norm_done, 1)
            nc.vector.memset(row_max[:], 0.0).then_inc(sm_free, 1)
            nc.vector.memset(neg_max[:], 0.0).then_inc(mrow_done, 1)
            nc.vector.memset(inv_l[0][:, 2:3], 0.0).then_inc(gated_done, 1)
            for i in range(RING):
                nc.vector.memset(inv_l[1][:, i:i + 1], 0.0).then_inc(pv_done, 1)
            for i in range(2):
                nc.vector.memset(v_all[:, i * H // 2:(i + 1) * H // 2, :, VW - 1], 1.0).then_inc(consts, 1)
            with dve.Fori(0, NB) as b:
                for u in range(NT):
                    n = b * 8 + 4 * u
                    dve.wait_ge(x_in[u], b * 32 + 16)
                    for g in range(TG):
                        nc.vector.bn_stats(stats[:, u, g, :], xt[u][:, g, :]).then_inc(bn_done, 1)
                    dve.wait_ge(bn_done, n + 4)
                    nc.vector.memset(waited[:], 0.0)
                    for g in range(TG):
                        nc.vector.bn_aggr(mv[:, u, g, :], stats[:, u, g, :]).then_inc(agg_done, 1)
                    dve.wait_ge(agg_done, n + 4)
                    nc.vector.tensor_scalar(var_eps[:, u, :], mv[:, u, :, 1], 1e-5, None, ALU.add).then_inc(var_done, 1)
                for u in range(NT):
                    dve.wait_ge(rstd_done, b * NT + u + 1)
                    for g in range(TG):
                        nc.vector.tensor_scalar(xt[u][:, g, :], xt[u][:, g, :], mv[:, u, g, 0:1], rstd[:, u, g:g + 1],
                                                ALU.subtract, ALU.mult).then_inc(x_ready, 1)
                for u in range(NT):
                    tok = slice(u * TILE, (u + 1) * TILE)
                    for fc in range(KC):
                        dve.wait_ge(r32_full, b * 32 + 12 * u + fc + 1)
                        split(b, 16 * u + fc, r32[fc % 4][:], h_hi[:, fc, :], h_lo[:, fc, :])
                    for c in range(2 * KC):
                        dve.wait_ge(r32_full, b * 32 + 12 * u + 4 + c + 1)
                        split(b, 16 * u + 4 + c, r32[c % 4][:], qk_hi[:, c, tok], qk_lo[:, c, tok])
                    for g in range(TG):
                        dve.wait_ge(wk_full, b * 32 + 12 * u + 8 + g + 1)
                        nc.vector.tensor_tensor(v32[g % 2][:], work(g), t["bv"][:], ALU.add).then_inc(v_add, 1)
                        dve.wait_ge(v_add, b * 8 + 4 * u + g + 1)
                        kc = TG * u + g
                        split(b, 16 * u + 12 + g, v32[g % 2][:].rearrange("p (h d) -> p h d", h=H),
                              v_all[:, :, kc, HD:2 * HD], v_all[:, :, kc, 0:HD])
                for i in range(GPB):
                    take_max(b, 0, i)
                negate_max(b, 0)
                for h in range(H):
                    for r in range(8):
                        if h + 1 < H:
                            for i in SM_AT[r]:
                                take_max(b, h + 1, i)
                                if i == 7:
                                    negate_max(b, h + 1)
                        if r == 0 and h:
                            low_part(b, h - 1, 7)
                            normalise(b, h - 1, 0)
                        if r == 4:
                            low_part(b, h, 3)
                            if h:
                                normalise(b, h - 1, 1)
                low_part(b, H - 1, 7)
                normalise(b, H - 1, 0)
                normalise(b, H - 1, 1)
                for u in range(NT):
                    for fc in range(KC):
                        dve.wait_ge(r32_full, b * 32 + 24 + 4 * u + fc + 1)
                        split(b, 32 + 4 * u + fc, r32[fc % 4][:], h_hi[:, fc, :], h_lo[:, fc, :])
                    for g in range(TG):
                        dve.wait_ge(wk_full, b * 32 + 24 + 4 * u + g + 1)
                        nc.vector.tensor_tensor(gated[g % 2][:], work(g), gate[:, 0, :], ALU.mult).then_inc(gated_done, 1)
                        dve.wait_ge(gated_done, b * 8 + 4 * u + g + 2)
                        dve.wait_ge(x_biased, b * 8 + 4 * u + g + 1)
                        nc.vector.tensor_tensor(xt[u][:, g, :], gated[g % 2][:], xt[u][:, g, :], ALU.add).then_inc(x1_ready, 1)


def load_weights(nc, ctx, t, dram):
    NSTG = 6
    stage = [ctx.enter_context(nc.sbuf_tensor(f"wstage{i}", [P, KC * D], F32)) for i in range(NSTG)]
    stage_in = [ctx.enter_context(nc.semaphore(f"wstage_in{i}")) for i in range(NSTG)]
    hi_done = ctx.enter_context(nc.semaphore("w_hi_done"))
    lo_done = ctx.enter_context(nc.semaphore("w_lo_done"))
    copied = ctx.enter_context(nc.semaphore("x1_copied"))

    with nc.Block() as block:

        @block.sync
        def _(sp):
            for n in range(N_FF_UNITS):
                if n >= NSTG:
                    sp.wait_ge(lo_done, n - NSTG + 1)
                sp.dma_start(stage[n % NSTG][:], dram["w"][N_ATT_UNITS + n]).then_inc(stage_in[n % NSTG], 16)
            sp.dma_start(dram["x1"][NB * NT:(NB + 1) * NT], dram["x1"][0:NT]).then_inc(copied, 16)
            sp.wait_ge(copied, 16)

        @block.scalar
        def _(act):
            for n in range(N_FF_UNITS):
                act.wait_ge(stage_in[n % NSTG], 16 * (n // NSTG + 1))
                nc.scalar.copy(t["wf_hi"][:, n].rearrange("p k n -> p (k n)"), stage[n % NSTG][:]).then_inc(hi_done, 1)

        @block.vector
        def _(dve):
            for n in range(N_FF_UNITS):
                dve.wait_ge(hi_done, n + 1)
                nc.vector.tensor_tensor(t["wf_lo"][:, n].rearrange("p k n -> p (k n)"), stage[n % NSTG][:],
                                        t["wf_hi"][:, n].rearrange("p k n -> p (k n)"), ALU.subtract).then_inc(lo_done, 1)


def feed_forward(nc, ctx, t, dram):
    def sb(name, shape, dt):
        return ctx.enter_context(nc.sbuf_tensor(name, shape, dt))

    def sem(name):
        return ctx.enter_context(nc.semaphore(name))

    xt = [sb(f"fx{u}", [P, TG, D], F32) for u in range(NT)]
    xn = sb("xn", [P, TG, D], F32)
    stats = sb("fstats", [P, TG, 6], F32)
    mv = sb("fmv", [P, TG, 2], F32)
    var_eps = sb("fvar_eps", [P, TG], F32)
    rstd = sb("frstd", [P, TG], F32)
    h_hi = [sb(f"fh_hi{u}", [P, KC, TILE], F16) for u in range(NT)]
    h_lo = [sb(f"fh_lo{u}", [P, KC, TILE], BF16) for u in range(NT)]
    r32 = [sb(f"fr32_{i}", [P, TILE], F32) for i in range(4)]
    a_hi = [sb(f"a_hi{i}", [P, TILE], F16) for i in range(4)]
    a_lo = [sb(f"a_lo{i}", [P, TILE], BF16) for i in range(4)]
    gate = [sb(f"fgate{s}", [P, 2, D], F32) for s in range(3)]
    gated = [sb(f"fgated{i}", [P, D], F32) for i in range(2)]
    waited = sb("fwaited", [P, 1], F32)
    mask_b = sb("mask_b", [P, GPB], F32)
    ln_ab = sb("ln_ab", [P, 2, 4, KC], F32)
    gb_masked = sb("gb_masked", [P, D], F32)

    tp = [ctx.enter_context(nc.psum_tensor(f"tp{i}", [P, TILE], F32)) for i in range(2)]
    hid = [ctx.enter_context(nc.psum_tensor(f"hid{i}", [P, TILE], F32)) for i in range(2)]
    acc = [ctx.enter_context(nc.psum_tensor(f"acc{g}", [P, D], F32)) for g in range(TG)]

    NCALL = 3 * NT
    site_of = [c // NT for c in range(NCALL)]
    chunks = [SITES[s]["chunks"] for s in site_of]
    before = [sum(chunks[:c]) for c in range(NCALL)]
    PER_BATCH = sum(chunks)
    assert all(m % 4 == 0 for m in chunks)
    ENTRIES = PER_BATCH + 4 * NCALL

    def hidden_entry(c, m):
        return 4 + before[c] + 4 * c + (m if m < chunks[c] - 1 else m + 2)

    def norm_entry(c, fc):
        return fc if c == 0 else 4 + before[c - 1] + 4 * (c - 1) + chunks[c - 1] - 1 + (fc if fc < 2 else fc + 1)

    x_in = [sem(f"fx_in{u}") for u in range(NT)]
    gate_in = [sem(f"fgate_in{s}") for s in range(3)]
    bn_done = sem("fbn_done")
    agg_done = sem("fagg_done")
    var_done = sem("fvar_done")
    rstd_done = sem("frstd_done")
    xn_ready = sem("xn_ready")
    tp_full = sem("ftp_full")
    hid_full = sem("hid_full")
    r32_full = sem("fr32_full")
    split_hi = sem("fsplit_hi")
    split_done = sem("fsplit_done")
    down_done = sem("down_done")
    acc_full = sem("acc_full")
    acc_free = sem("acc_free")
    x_biased = sem("fx_biased")
    mask_ready = sem("mask_ready")
    gb_done = sem("gb_done")
    x_new = sem("x_new")
    out_done = [sem(f"out_done{u}") for u in range(NT)]
    sp_turn = sem("fsp_turn")
    act_turn = sem("act_turn")
    abc_ready = sem("abc_ready")
    consts = sem("fconsts")

    with nc.Block() as block:

        @block.sync
        def _(sp):
            def wait(sem_, value):
                sp.wait_ge(sem_, sp.snap(value))
                sp.sem_inc(sp_turn, 1)

            def load(u, tile):
                sp.dma_start(xt[u][:], dram["x1"][bass.ds(tile, 1)].rearrange("t p g n -> p (t g) n")).then_inc(x_in[u], 16)

            for u in range(NT):
                sp.dma_start(xt[u][:], dram["x1"][u]).then_inc(x_in[u], 16)
            for s in range(3):
                sp.dma_start(gate[s][:], dram["gates"][1 + s, 0:1].rearrange("b k n -> (b k n)").partition_broadcast(P)).then_inc(gate_in[s], 16)
            with sp.Fori(0, NB) as b:
                for s in range(3):
                    if s == 2:
                        wait(x_new, b * 24 + 20)
                        sp.dma_start(dram["out"][bass.ds(b * NT, 1)].rearrange("t p g n -> p (t g) n"), xt[0][:]).then_inc(out_done[0], 16)
                        wait(out_done[0], b * 16 + 16)
                        load(0, b * NT + NT)
                    wait(x_new, b * 24 + 8 * s + 8)
                    sp.dma_start(gate[s][:], dram["gates"][1 + s, bass.ds(b + 1, 1)].rearrange("b k n -> (b k n)").partition_broadcast(P)).then_inc(gate_in[s], 16)
                sp.dma_start(dram["out"][bass.ds(b * NT + 1, 1)].rearrange("t p g n -> p (t g) n"), xt[1][:]).then_inc(out_done[1], 16)
                wait(out_done[1], b * 16 + 16)
                load(1, b * NT + NT + 1)
            for u in range(NT):
                sp.wait_ge(x_in[u], 16 * (NB + 1))
            for s in range(3):
                sp.wait_ge(gate_in[s], 16 * (NB + 1))

        @block.tensor
        def _(pe):
            wf = (t["wf_hi"], t["wf_lo"])

            def transpose_chunk(b, c, fc):
                if fc == 0:
                    pe.wait_ge(xn_ready, b * 24 + 4 * c + 4)
                if fc >= 2:
                    pe.wait_ge(r32_full, b * ENTRIES + norm_entry(c, fc - 2) + 1)
                for g in range(TG):
                    mm = nc.tensor.transpose(tp[fc % 2][:, g * P:(g + 1) * P], xn[:, g, fc * P:(fc + 1) * P], t["ident"][:])
                mm.then_inc(tp_full, 1)

            def up(b, c, m):
                u, un, col = c % NT, SITES[site_of[c]]["up"] + m // KC, m % KC * P
                if m == 0:
                    pe.wait_ge(split_done, b * ENTRIES + norm_entry(c, 3) + 1)
                if m >= 2:
                    pe.wait_ge(r32_full, b * ENTRIES + hidden_entry(c, m - 2) + 1)
                elif c:
                    pe.wait_ge(r32_full, b * ENTRIES + hidden_entry(c - 1, chunks[c - 1] - 2 + m) + 1)
                for kc in range(KC):
                    for k, (w, a) in enumerate(((wf[0], h_hi), (wf[0], h_lo), (wf[1], h_hi))):
                        mm = nc.tensor.matmul(hid[m % 2][:], w[:, un, kc, col:col + P], a[u][:, kc, :],
                                              start=(kc == 0 and k == 0), stop=(kc == KC - 1 and k == 2))
                mm.then_inc(hid_full, 1)

            def down(b, c, m):
                un, kc = SITES[site_of[c]]["down"] + m // KC, m % KC
                pe.wait_ge(split_done, b * ENTRIES + hidden_entry(c, m) + 1)
                last = m == chunks[c] - 1
                for g in range(TG):
                    if m == 0:
                        pe.wait_ge(acc_free, b * 24 + 4 * c + g + 1)
                    for k, (a, w) in enumerate(((a_hi, wf[0]), (a_hi, wf[1]), (a_lo, wf[0]))):
                        mm = nc.tensor.matmul(acc[g][:], a[m % 4][:, g * P:(g + 1) * P], w[:, un, kc, :],
                                              start=(m == 0 and k == 0), stop=(last and k == 2))
                    if last and g < TG - 1:
                        mm.then_inc(acc_full, 1)
                mm.then_inc(down_done, 1)

            pe.wait_ge(consts, 1)
            for fc in range(KC):
                transpose_chunk(0, 0, fc)
            with pe.Fori(0, NB) as b:
                for c in range(NCALL):
                    n = chunks[c]
                    for m in range(n):
                        up(b, c, m)
                        if m == n - 1:
                            transpose_chunk(b, c + 1, 2)
                            transpose_chunk(b, c + 1, 3)
                        if m >= 2:
                            down(b, c, m - 2)
                        if m == n - 2:
                            transpose_chunk(b, c + 1, 0)
                            transpose_chunk(b, c + 1, 1)
                    down(b, c, n - 2)
                    down(b, c, n - 1)

        @block.scalar
        def _(act):
            def entry(b, n, src, func, bias, scale=1.0):
                if not isinstance(n, int) or n >= 4 or not isinstance(b, int):
                    act.wait_ge(split_done, b * ENTRIES + n - 3)
                nc.scalar.activation(r32[n % 4][:], src, func, bias=bias, scale=scale).then_inc(r32_full, 1)

            def norm_chunk(b, c, fc):
                k = site_of[c] if c < NCALL else 3
                act.wait_ge(tp_full, b * 24 + 4 * c + fc + 1)
                entry(b, norm_entry(c, fc), tp[fc % 2][:], ACT.Identity, ln_ab[:, 1, k, fc:fc + 1],
                      ln_ab[:, 0, k, fc:fc + 1])

            act.wait_ge(consts, 1)
            for k, ab in enumerate((t["ln_a"], t["ln_b"])):
                nc.scalar.copy(ln_ab[:, k, 0, :], ab[:, 1, :, 0]).then_inc(abc_ready, 2)
            act.wait_ge(abc_ready, 4)
            for fc in range(KC):
                norm_chunk(0, 0, fc)
            with act.Fori(0, NB) as b:
                act.wait_ge(r32_full, b * ENTRIES + 4)
                act.sem_inc(act_turn, 1)
                for k, ab in enumerate((t["ln_a"], t["ln_b"])):
                    nc.scalar.copy(ln_ab[:, k, 0:3, :], ab[:, 1:4, :, bass.ds(b, 1)]).then_inc(abc_ready, 1)
                    nc.scalar.copy(ln_ab[:, k, 3, :], ab[:, 1, :, bass.ds(b + 1, 1)]).then_inc(abc_ready, 1)
                act.wait_ge(abc_ready, b * 4 + 8)
                for c in range(NCALL):
                    n, s = chunks[c], SITES[site_of[c]]
                    for m in range(n):
                        if m == n - 1:
                            norm_chunk(b, c + 1, 0)
                            norm_chunk(b, c + 1, 1)
                        col = C_UP + s["bias"] + m
                        act.wait_ge(hid_full, b * PER_BATCH + before[c] + m + 1)
                        entry(b, hidden_entry(c, m), hid[m % 2][:], s["act"], t["cols"][:, col:col + 1])
                    norm_chunk(b, c + 1, 2)
                    norm_chunk(b, c + 1, 3)

        @block.gpsimd
        def _(pool):
            def inverse_deviation(n):
                pool.wait_ge(var_done, n + 1)
                nc.gpsimd.tensor_tensor(rstd[:], var_eps[:], t["minus_half"][:], ALU.pow).then_inc(rstd_done, 1)

            pool.wait_ge(consts, 1)
            inverse_deviation(0)
            with pool.Fori(0, NB) as b:
                nc.gpsimd.tensor_copy(mask_b[:], t["mask"][:, bass.ds(b * GPB, GPB)]).then_inc(mask_ready, 1)
                pool.wait_ge(mask_ready, b + 1)
                for c in range(NCALL):
                    s, u = site_of[c], c % NT
                    pool.wait_ge(gate_in[s], b * 16 + 16)
                    pool.wait_ge(xn_ready, b * 24 + 4 * c + 4)
                    for g in range(TG):
                        gb = gate[s][:, 1, :]
                        if s == 1:
                            pool.wait_ge(x_biased, b * 24 + 4 * c + g)
                            nc.gpsimd.tensor_tensor(gb_masked[:], gb, mask_b[:, TG * u + g:TG * u + g + 1].to_broadcast([P, D]),
                                                    ALU.mult).then_inc(gb_done, 1)
                            pool.wait_ge(gb_done, b * 8 + 4 * u + g + 1)
                            gb = gb_masked[:]
                        nc.gpsimd.tensor_tensor(xt[u][:, g, :], xt[u][:, g, :], gb, ALU.add).then_inc(x_biased, 1)
                    inverse_deviation(b * NCALL + (c + 1))

        @block.vector
        def _(dve):
            def split(b, n, hi, lo):
                dve.wait_ge(r32_full, b * ENTRIES + n + 1)
                nc.vector.tensor_copy(hi, r32[n % 4][:]).then_inc(split_hi, 1)
                dve.wait_ge(split_hi, b * ENTRIES + n + 1)
                nc.vector.tensor_tensor(lo, r32[n % 4][:], hi, ALU.subtract).then_inc(split_done, 1)

            def split_norm(b, c, fc):
                u = c % NT
                split(b, norm_entry(c, fc), h_hi[u][:, fc, :], h_lo[u][:, fc, :])

            def statistics(b, c, groups):
                u, n = c % NT, b * 24 + 4 * c
                eps = SITES[site_of[c] if c < NCALL else 0]["eps"]
                if groups[0] == 0 and c in (0, 1, NCALL):
                    dve.wait_ge(x_in[u], b * 16 + 16 * (1 + c // NCALL))
                elif groups[0] == 0:
                    dve.wait_ge(x_new, b * 24 + 4 * (c - NT) + 4)
                for g in groups:
                    nc.vector.bn_stats(stats[:, g, :], xt[u][:, g, :]).then_inc(bn_done, 1)
                if groups[-1] == TG - 1:
                    dve.wait_ge(bn_done, n + 4)
                    nc.vector.memset(waited[:], 0.0)
                    for g in range(TG):
                        nc.vector.bn_aggr(mv[:, g, :], stats[:, g, :]).then_inc(agg_done, 1)
                    dve.wait_ge(agg_done, n + 4)
                    nc.vector.tensor_scalar(var_eps[:], mv[:, :, 1], eps, None, ALU.add).then_inc(var_done, 1)

            def normalise(b, c):
                u = c % NT
                dve.wait_ge(rstd_done, b * NCALL + (c + 1))
                if not (isinstance(b, int) and c == 0):
                    dve.wait_ge(tp_full, b * 24 + 4 * c)
                for g in range(TG):
                    nc.vector.tensor_scalar(xn[:, g, :], xt[u][:, g, :], mv[:, g, 0:1], rstd[:, g:g + 1],
                                            ALU.subtract, ALU.mult).then_inc(xn_ready, 1)

            def residual(b, c):
                s, u = site_of[c], c % NT
                for g in range(TG):
                    k = b * 24 + 4 * c + g
                    if g < TG - 1:
                        dve.wait_ge(acc_full, b * 18 + 3 * c + g + 1)
                    else:
                        dve.wait_ge(down_done, b * PER_BATCH + before[c] + chunks[c] + 4)
                    if s == 1:
                        nc.vector.scalar_tensor_tensor(
                            out=gated[g % 2][:], in0=acc[g][:], scalar=mask_b[:, TG * u + g:TG * u + g + 1],
                            in1=gate[s][:, 0, :], op0=ALU.mult, op1=ALU.mult).then_inc(acc_free, 1)
                    else:
                        nc.vector.tensor_tensor(gated[g % 2][:], acc[g][:], gate[s][:, 0, :], ALU.mult).then_inc(acc_free, 1)
                    dve.wait_ge(acc_free, k + 1 + 4)
                    dve.wait_ge(x_biased, k + 1)
                    nc.vector.tensor_tensor(xt[u][:, g, :], gated[g % 2][:], xt[u][:, g, :], ALU.add).then_inc(x_new, 1)

            for i in range(4):
                nc.vector.memset(gated[0][:, i:i + 1], 0.0).then_inc(down_done, 1)
            for i in range(4):
                nc.vector.memset(gated[0][:, 4 + i:5 + i], 0.0).then_inc(acc_free, 1)
            nc.vector.memset(gb_masked[:], 0.0).then_inc(consts, 1)
            statistics(0, 0, range(TG))
            normalise(0, 0)
            for fc in range(KC):
                split_norm(0, 0, fc)
            with dve.Fori(0, NB) as b:
                for c in range(NCALL):
                    n = chunks[c]
                    for m in range(n):
                        if m == n - 1:
                            split_norm(b, c + 1, 0)
                            split_norm(b, c + 1, 1)
                        dve.wait_ge(down_done, b * PER_BATCH + before[c] + m + 1)
                        split(b, hidden_entry(c, m), a_hi[m % 4][:], a_lo[m % 4][:])
                        if m == n - 5:
                            statistics(b, c + 1, range(0, 2))
                        if m == n - 4:
                            statistics(b, c + 1, range(2, TG))
                        if m == n - 3:
                            normalise(b, c + 1)
                    split_norm(b, c + 1, 2)
                    split_norm(b, c + 1, 3)
                    residual(b, c)


def build(nc, dram):
    with ExitStack() as ctx:
        def sb(name, shape, dt, to=ctx):
            return to.enter_context(nc.sbuf_tensor(name, shape, dt))

        t = dict(
            cols=sb("cols", [P, NCOLS], F32),
            ident=sb("ident", [P, P], F32),
            ident16=sb("ident16", [P, P], F16),
            mask=sb("mask", [P, NB * GPB], F32),
            minus_half=sb("minus_half", [P, TG], F32),
            ln_a=sb("ln_a", [P, 4, KC, NB + 1], F32),
            ln_b=sb("ln_b", [P, 4, KC, NB + 1], F32),
        )
        with ExitStack() as att:
            t["bv"] = sb("bv", [P, D], F32, att)
            t["wa_hi"] = sb("wa_hi", [P, N_ATT_UNITS, KC, D], F16, att)
            t["wa_lo"] = sb("wa_lo", [P, N_ATT_UNITS, KC, D], BF16, att)
            with ExitStack() as s:
                prologue(nc, s, t, dram)
            with ExitStack() as s:
                attention(nc, s, t, dram)
        t["wf_hi"] = sb("wf_hi", [P, N_FF_UNITS, KC, D], F16)
        t["wf_lo"] = sb("wf_lo", [P, N_FF_UNITS, KC, D], BF16)
        with ExitStack() as s:
            load_weights(nc, s, t, dram)
        with ExitStack() as s:
            feed_forward(nc, s, t, dram)


def kernel(**inputs):
    import concourse.bacc as bacc
    from concourse.bass_utils import run_bass_kernel_spmd as run

    a = {k: np.asarray(v) for k, v in inputs.items()}

    def units(w):
        r, c = w.shape[0] // D, w.shape[1] // D
        return w.reshape(r, KC, P, c, D).transpose(0, 3, 2, 1, 4).reshape(r * c, P, KC * D)

    def columns(v):
        return v.reshape(-1, P).T

    ada_b = [a["L0_cond_bt"][0:3 * D], a["L0_cond_bt"][3 * D:6 * D], a["L1_cond_ada_b"], a["L1_cond_ffada_b"]]
    arrays = {
        "x": a["x"],
        "condT": a["cond_1024"].reshape(NB, KC, P).transpose(2, 1, 0),
        "mask": np.ascontiguousarray(a["mask_BxS_bk0"].reshape(NB * GPB, P).T),
        "ident": np.eye(P, dtype=np.float32),
        "ada": np.concatenate([units(a["L0_cond_Wt"]), units(a["L1_cond_ada_w"]), units(a["L1_cond_ffada_w"])]),
        "w": np.concatenate([units(a[k]) for k in (
            "L0_cond_Wqkv", "L0_cond_Wproj", "L0_cond_W1", "L0_cond_W2", "L1_cond_ssm_w1", "L1_cond_bwd_w1",
            "L1_cond_ssm_w2", "L1_cond_bwd_w2", "L1_cond_ff_w1", "L1_cond_ff_w2")]),
        "cols": np.concatenate([columns(v) for v in (
            *[b[0:2 * D] for b in ada_b], a["L0_cond_g1"], a["L0_cond_be1"], a["L0_cond_g2"], a["L0_cond_be2"],
            a["L0_cond_bqkv"][0:2 * D], a["L0_cond_b1"], a["L1_cond_ssm_b1"], a["L1_cond_bwd_b1"],
            a["L1_cond_ff_b1"])], axis=1),
        "rows": np.stack([*[b[2 * D:3 * D] for b in ada_b], a["L0_cond_bproj"], a["L0_cond_b2"], a["L1_cond_ssm_b2"],
                          a["L1_cond_ff_b2"], a["L1_cond_bwd_b2"], a["L0_cond_bqkv"][2 * D:3 * D]]),
    }
    arrays = {k: np.ascontiguousarray(v) for k, v in arrays.items()}

    nc = bacc.Bacc("TRN2", target_bir_lowering=False, num_devices=1)
    dram = {k: nc.dram_tensor("in_" + k, v.shape, mybir.dt.from_np(v.dtype), kind="ExternalInput").ap() for k, v in arrays.items()}
    out = nc.dram_tensor("out", (NB, L, D), F32, kind="ExternalOutput").ap()
    rows = "b (u g p) n -> (b u) p g n"
    dram["x"] = dram["x"].rearrange(rows, u=NT, g=TG)
    dram["out"] = out.rearrange(rows, u=NT, g=TG)
    dram["x1"] = nc.dram_tensor("x1_dram", (NB * NT + NT, P, TG, D), F32, kind="Internal").ap()
    dram["gates"] = nc.dram_tensor("gates_dram", (4, NB + 1, 2, D), F32, kind="Internal").ap()
    build(nc, dram)
    r = run(nc, [{"in_" + k: v for k, v in arrays.items()}], core_ids=[0])
    return r.results[0]["out"]
```

```python
from contextlib import ExitStack

import numpy as np

import concourse.bass as bass
from concourse import mybir

F32 = mybir.dt.float32
F16 = mybir.dt.float16
BF16 = mybir.dt.bfloat16
U8 = mybir.dt.uint8
ALU = mybir.AluOpType
ACT = mybir.ActivationFunctionType
AX_X = mybir.AxisListType.X

P = 128
NB = 4
L = 1024
D = 512
H = 16
HD = D // H
KC = D // P
TILE = 512
TG = TILE // P
NT = L // TILE
GPB = L // P
SCALE = float(HD) ** -0.5
M_UNIT = 64.0
VW = 2 * HD + 1
VP = VW + 1
STACK = 3 * HD

U_QKV, U_PROJ = 0, 3
N_ATT_UNITS = 4
N_FF_UNITS = 16
SITES = [
    dict(chunks=16, up=0, down=4, eps=1e-5, bias=0, act=ACT.Gelu),
    dict(chunks=8, up=8, down=10, eps=1e-6, bias=16, act=ACT.Gelu),
    dict(chunks=8, up=12, down=14, eps=1e-6, bias=24, act=ACT.Gelu_apprx_tanh),
]
C_ADA = 0
C_G1, C_BE1, C_G2, C_BE2 = 32, 36, 40, 44
C_QK = 48
C_UP = 56
C_V = 88
NCOLS = 92
R_GATE, R_OUT, R_BWD = 0, 4, 8
NROWS = 9

NST = 4
RING = 4
R32 = 2
LAG = 3
DVE_PAIRS = (3, 7)
SM_HALVES = 2 * GPB
SM_AT = ((0, 1, 2), (3, 4, 5), (6, 7), (8, 9), (10, 11), (12, 13), (14, 15), ())
ROW_AT = 7
POOL_PAIRS = tuple(r for r in range(8) if r not in DVE_PAIRS)


def prologue(nc, ctx, t, dram):
    def sb(name, shape, dt):
        return ctx.enter_context(nc.sbuf_tensor(name, shape, dt))

    def sem(name):
        return ctx.enter_context(nc.semaphore(name))

    NSTG = 8
    stage = [sb(f"stage{i}", [P, KC, D], F32) for i in range(NSTG)]
    condT = sb("condT", [P, KC, NB], F32)
    sil = sb("sil", [P, KC, NB], F32)
    vec = sb("vec", [P, 4, 2, KC, NB], F32)
    one_plus = sb("one_plus", [P, 4, KC, NB], F32)
    rows4 = sb("rows4", [NB, NROWS, D], F32)
    gates = sb("gates", [NB, 4, 2, D], F32)
    mask_u8 = sb("mask_u8", [P, NB * GPB], U8)
    p_vec = [ctx.enter_context(nc.psum_tensor(f"p_vec{i}", [P, D], F32)) for i in range(4)]
    pv = [p[:, 0:2 * KC * NB].rearrange("p (k m b) -> p k m b", k=2, m=KC) for p in p_vec]
    bv4 = sb("bv4", [P, KC, NB], F32)
    p_bv = ctx.enter_context(nc.psum_tensor("p_bv", [P, D], F32))
    pg = [ctx.enter_context(nc.psum_tensor(f"p_gate{i}", [P, D], F32)) for i in range(2)]

    small_in = sem("small_in")
    stage_in = [sem(f"stage_in{i}") for i in range(NSTG)]
    sil_done = sem("sil_done")
    unit_used = sem("unit_used")
    vec_step = sem("vec_step")
    gate_read = sem("gate_read")
    gates_out = sem("gates_out")
    x_landed = sem("x_landed")
    hi_done = sem("hi_done")
    lo_done = sem("lo_done")
    bv_rep = sem("bv_rep")
    turns = [("att", U_PROJ)] + [("ada", u) for u in range(3)] + [("att", u) for u in range(U_PROJ)] + \
            [("ada", u) for u in range(3, 12)]
    att_units = [(n, u) for n, (kind, u) in enumerate(turns) if kind == "att"]
    ada_units = [(n, u) for n, (kind, u) in enumerate(turns) if kind == "ada"]

    with nc.Block() as block:

        @block.sync
        def _(sp):
            sp.dma_start(condT[:], dram["condT"]).then_inc(small_in, 16)
            sp.dma_start(t["cols"][:], dram["cols"]).then_inc(small_in, 16)
            sp.dma_start(t["ident"][:], dram["ident"]).then_inc(small_in, 16)
            sp.dma_start(mask_u8[:], dram["mask"]).then_inc(small_in, 16)
            sp.dma_start(rows4[:].rearrange("b r n -> b (r n)"),
                         dram["rows"].rearrange("r n -> (r n)").partition_broadcast(NB)).then_inc(small_in, 16)
            for n, (kind, u) in enumerate(turns):
                if n >= NSTG:
                    old = turns[n - NSTG]
                    if old[0] == "att":
                        sp.wait_ge(lo_done, att_units.index((n - NSTG, old[1])) + 1)
                    if old[0] == "ada" or old[1] == U_PROJ:
                        sp.wait_ge(unit_used, old[1] + 2 if old[0] == "ada" else 1)
                src = dram["w" if kind == "att" else "ada"][u]
                sp.dma_start(stage[n % NSTG][:].rearrange("p k n -> p (k n)"), src).then_inc(stage_in[n % NSTG], 16)
            for u in range(NT):
                sp.dma_start(t["xt"][u][:], dram["x"][NT + u]).then_inc(x_landed, 16)
            sp.wait_ge(gate_read, 4)
            for s in range(4):
                first, spare = (1, 0) if s == 0 else (0, NB)
                sp.dma_start(dram["gates"][s, first:first + NB], gates[:, s]).then_inc(gates_out, 16)
                sp.dma_start(dram["gates"][s, spare:spare + 1], gates[0:1, s]).then_inc(gates_out, 16)
            sp.wait_ge(gates_out, 8 * 16)
            sp.wait_ge(x_landed, 16 * NT)

        @block.scalar
        def _(act):
            act.wait_ge(small_in, 80)
            nc.scalar.activation(sil[:], condT[:], ACT.Silu).then_inc(sil_done, 1)
            for n, u in att_units:
                act.wait_ge(stage_in[n % NSTG], 16 * (n // NSTG + 1))
                nc.scalar.copy(t["wa_hi"][:, u], stage[n % NSTG][:]).then_inc(hi_done, 1)

        @block.tensor
        def _(pe):
            pe.wait_ge(bv_rep, 1)
            pe.wait_ge(stage_in[0], 16)
            for kc in range(KC):
                mm = nc.tensor.matmul(p_bv[0:NB, :], bv4[:, kc, :], stage[0][:, kc, :], start=(kc == 0), stop=(kc == KC - 1))
            mm.then_inc(unit_used, 1)
            pe.wait_ge(sil_done, 1)
            for n, unit in ada_units:
                site, part = divmod(unit, 3)
                w = stage[n % NSTG]
                pe.wait_ge(stage_in[n % NSTG], 16 * (n // NSTG + 1))
                if part < 2:
                    for m in range(KC):
                        for kc in range(KC):
                            mm = nc.tensor.matmul(pv[site][:, part, m, :], w[:, kc, m * P:(m + 1) * P], sil[:, kc, :],
                                                  start=(kc == 0), stop=(kc == KC - 1))
                else:
                    if site >= 2:
                        pe.wait_ge(gate_read, site - 1)
                    for kc in range(KC):
                        mm = nc.tensor.matmul(pg[site % 2][0:NB, :], sil[:, kc, :], w[:, kc, :],
                                              start=(kc == 0), stop=(kc == KC - 1))
                mm.then_inc(unit_used, 1)

        @block.vector
        def _(dve):
            step = 0

            def then(ins):
                nonlocal step
                step += 1
                ins.then_inc(vec_step, 1)
                dve.wait_ge(vec_step, step)

            def low_of_unit(n, u):
                dve.wait_ge(hi_done, att_units.index((n, u)) + 1)
                nc.vector.tensor_tensor(t["wa_lo"][:, u], stage[n % NSTG][:], t["wa_hi"][:, u],
                                        ALU.subtract).then_inc(lo_done, 1)

            cols = t["cols"]
            dve.wait_ge(small_in, 80)
            nc.vector.tensor_copy(bv4[:], cols[:, C_V:C_V + KC].unsqueeze(2).to_broadcast([P, KC, NB])).then_inc(bv_rep, 1)
            nc.vector.tensor_copy(t["ident16"][:], t["ident"][:])
            nc.vector.tensor_copy(t["mask"][:], mask_u8[:])
            then(nc.vector.tensor_tensor(rows4[:, R_OUT + 2, :], rows4[:, R_OUT + 2, :], rows4[:, R_BWD, :], ALU.add))
            for a in (t["ln_a"], t["ln_b"]):
                then(nc.vector.memset(a[:], 1.0))
            low_of_unit(*att_units[0])
            dve.wait_ge(unit_used, 1)
            then(nc.vector.tensor_tensor(rows4[:, R_OUT, :], p_bv[0:NB, :], rows4[:, R_OUT, :], ALU.add))
            for site in range(4):
                dve.wait_ge(unit_used, 3 * site + 4)
                then(nc.vector.tensor_tensor(
                    vec[:, site], pv[site],
                    cols[:, C_ADA + 8 * site:C_ADA + 8 * site + 8].rearrange("p (k m) -> p k m", k=2)
                    .unsqueeze(3).to_broadcast([P, 2, KC, NB]), ALU.add))
                a, b = t["ln_a"][:, site, :, 0:NB], t["ln_b"][:, site, :, 0:NB]
                if site < 2:
                    g = cols[:, (C_G1, C_G2)[site]:(C_G1, C_G2)[site] + KC].unsqueeze(2).to_broadcast([P, KC, NB])
                    be = cols[:, (C_BE1, C_BE2)[site]:(C_BE1, C_BE2)[site] + KC].unsqueeze(2).to_broadcast([P, KC, NB])
                    then(nc.vector.tensor_scalar(one_plus[:, site], vec[:, site, 1], 1.0, None, ALU.add))
                    then(nc.vector.tensor_tensor(a, one_plus[:, site], g, ALU.mult))
                    then(nc.vector.tensor_tensor(b, one_plus[:, site], be, ALU.mult))
                    then(nc.vector.tensor_tensor(b, b, vec[:, site, 0], ALU.add))
                else:
                    then(nc.vector.tensor_scalar(a, vec[:, site, 1], 1.0, None, ALU.add))
                    then(nc.vector.tensor_copy(b, vec[:, site, 0]))
                then(nc.vector.tensor_tensor(gates[:, site, 0, :], pg[site % 2][0:NB, :], rows4[:, R_GATE + site, :], ALU.add))
                nc.vector.tensor_tensor(gates[:, site, 1, :], gates[:, site, 0, :], rows4[:, R_OUT + site, :],
                                        ALU.mult).then_inc(gate_read, 1)
                if site == 0:
                    for n, u in att_units[1:]:
                        low_of_unit(n, u)


def attention(nc, ctx, t, dram):
    def sb(name, shape, dt):
        return ctx.enter_context(nc.sbuf_tensor(name, shape, dt))

    def sem(name):
        return ctx.enter_context(nc.semaphore(name))

    xt = t["xt"]
    xr = [sb(f"xr{i}", [P, D], F32) for i in range(4)]
    stats = sb("stats", [P, NT, TG, 6], F32)
    mv = sb("mv", [P, NT, TG, 2], F32)
    var_eps = sb("var_eps", [P, NT, TG], F32)
    rstd = sb("rstd", [P, NT, TG], F32)
    h_hi = [sb(f"h_hi{u}", [P, KC, TILE], F16) for u in range(NT)]
    h_lo = [sb(f"h_lo{u}", [P, KC, TILE], BF16) for u in range(NT)]
    r32 = [sb(f"r32_{i}", [P, TILE], F32) for i in range(R32)]
    qk_hi = sb("qk_hi", [P, 2 * KC, L], F16)
    qk_lo = sb("qk_lo", [P, 2 * KC, L], F16)
    v_all = sb("v_all", [P, H, GPB, VP], F16)
    v_last = sb("v_last", [P, 4, GPB, VP], F16)
    q_st = [sb(f"q_st{e}", [P, L], F16) for e in range(NST)]
    k_st = [sb(f"k_st{e}", [P, L], F16) for e in range(NST)]
    p32 = [sb(f"p32_{i}", [P, 2, TILE], F32) for i in range(RING)]
    p_lo = [sb(f"p_lo{i}", [P, 2, TILE], F16) for i in range(RING)]
    half_max = sb("half_max", [P, 2, GPB, 2], F32)
    row_max = sb("row_max", [P, 2, GPB], F32)
    neg_max = sb("neg_max", [P, 2, GPB], F16)
    raw = [sb(f"raw{i}", [P, TG, VW], F32) for i in range(2)]
    o_sum = [sb(f"o_sum{i}", [P, TG, HD], F32) for i in range(2)]
    inv_l = [sb(f"inv_l{i}", [P, TG], F32) for i in range(2)]
    o_rows = sb("o_rows", [P, GPB, D], F32)
    gate = sb("gate_att", [P, 2, D], F32)
    gated = [sb(f"gated{i}", [P, D], F32) for i in range(2)]
    waited = sb("waited", [P, 1], F32)
    ln_ab = sb("ln_ab_att", [P, 2, KC], F32)

    s_max = [ctx.enter_context(nc.psum_tensor(f"s_max{i}", [P, TILE], F32)) for i in range(3)]
    s_exp = [ctx.enter_context(nc.psum_tensor(f"s_exp{i}", [P, TILE], F32)) for i in range(2)]
    pv = ctx.enter_context(nc.psum_tensor("pv", [P, TG, P], F32))
    bg = [ctx.enter_context(nc.psum_tensor(f"bg{i}", [P, TILE], F32)) for i in range(2)]

    def work(i):
        return (*s_max, bg[1])[i][:]

    places = {1: [("p", 0), ("p", 1), ("p", 2)], 2: [("p", 3), ("p", 4), ("p", 5)], 3: [("p", 6), ("p", 7)],
              5: [("qk", 0, 0), ("qk", 4, 0), ("qk", 0, 1)], 6: [("qk", 4, 1), ("qk", 1, 0), ("qk", 5, 0)],
              7: [("qk", 1, 1)], 8: [("qk", 5, 1)],
              9: [("v", 0, 0), ("v", 0, 1)], 10: [("qk", 2, 0), ("qk", 6, 0), ("v", 0, 2)],
              11: [("qk", 2, 1), ("qk", 6, 1)], 12: [("v", 0, 3)],
              13: [("v", 1, 0), ("v", 1, 1), ("v", 1, 2)], 14: [("v", 1, 3), ("qk", 3, 0), ("qk", 7, 0)],
              15: [("qk", 3, 1), ("qk", 7, 1)]}
    dense = {}
    order = []
    for h in range(H):
        for r in range(8):
            if h in (0, 4):
                dense[h, r] = (("o" if h == 0 else "x", r // 4, r % 4), 0, 1)
            elif h in places and r % 3 < 2 and r // 3 < len(places[h]):
                dense[h, r] = (places[h][r // 3], r % 3, 2)
            if (h, r) in dense and dense[h, r][1] == 0:
                order.append(dense[h, r][0])
    NBG = len(order)
    bg_at = {task: n for n, task in enumerate(order)}
    split_order = [task for task in order if task[0] != "p"]
    NSP = len(split_order)
    sp_at = {task: n for n, task in enumerate(split_order)}
    assert NBG == 48 and NSP == 40

    x_in = [sem(f"x_in{u}") for u in range(NT)]
    bn_done = sem("bn_done")
    agg_done = sem("agg_done")
    var_done = sem("var_done")
    rstd_done = sem("rstd_done")
    x_ready = sem("x_ready")
    bg_full = sem("bg_full")
    bg_hi = sem("bg_hi")
    gated_done = sem("gated_done")
    bg_lo = sem("bg_lo")
    stack_in = [sem(f"stack_in{e}") for e in range(NST)]
    v_in = sem("v_in")
    sm_full = sem("sm_full")
    sm_free = sem("sm_free")
    both_done = sem("both_done")
    max_done = sem("max_done")
    mrow_full = sem("mrow_full")
    mrow_done = sem("mrow_done")
    st_full = sem("st_full")
    exp_done = sem("exp_done")
    lo_pool = sem("lo_pool")
    lo_dve = sem("lo_dve")
    pv_done = sem("pv_done")
    raw_done = sem("raw_done")
    inv_done = sem("inv_done")
    sum_done = sem("sum_done")
    o_ready = sem("o_ready")
    gate_in = sem("gate_in")
    xr_in = [sem(f"xr_in{i}") for i in range(4)]
    x_biased = sem("x_biased")
    x1_ready = sem("x1_ready")
    x1_out = [sem(f"x1_out{i}") for i in range(4)]
    ab_ready = sem("ab_ready")
    sp_turn = sem("sp_turn")
    consts = sem("consts")
    k_rows = sem("k_rows")
    tp_full = sem("tp_full")
    wk_full = sem("wk_full")
    r_hi = sem("r_hi")
    r_lo = sem("r_lo")
    wk_free = sem("wk_free")

    NPL, NDV = len(POOL_PAIRS), len(DVE_PAIRS)
    HEAD_DMAS = 6
    HEADS_OF_SLOT = H // NST
    R_TILE = KC + 3 * KC
    R_END = NT * R_TILE

    def filled(h, r, slots):
        h, r = divmod(8 * h + r - slots, 8)
        task, part, parts = dense.get((h, r), (None, 0, 0))
        return task if part == parts - 1 else None

    def done_in_last(task):
        return task[0] in ("o", "p")

    def v_places(half, j, lo_part):
        d = slice(0, HD) if lo_part else slice(HD, 2 * HD)
        kc = slice(2 * j, 2 * j + 2)
        if half == 0:
            places = [(slice(0, 8), v_all[:, 0:8, kc, d])]
        else:
            places = [(slice(0, 4), v_all[:, 8:12, kc, d]), (slice(4, 8), v_last[:, :, kc, d])]
        return [(heads, x.rearrange("p h c d -> p c h d")) for heads, x in places]

    def by_heads(x):
        return x.rearrange("p (c h d) -> p c h d", c=2, d=HD)

    with nc.Block() as block:

        @block.sync
        def _(sp):
            def wait(sem_, value):
                sp.wait_ge(sem_, value if isinstance(value, int) else sp.snap(value))
                sp.sem_inc(sp_turn, 1)

            def load_stacks(h):
                g, j, e = h % H // 4, h % 4, h % NST
                part = slice(j * HD, (j + 1) * HD)
                for dst, at, src, chunk in ((q_st, 0, qk_hi, g), (q_st, 1, qk_lo, g), (q_st, 2, qk_hi, g),
                                            (k_st, 0, qk_hi, KC + g), (k_st, 1, qk_hi, KC + g),
                                            (k_st, 2, qk_lo, KC + g)):
                    sp.dma_start(dst[e][at * HD:(at + 1) * HD, :], src[part, chunk, :]).then_inc(stack_in[e], 16)

            def token_group(name, b, n):
                return dram[name][bass.ds(b * NT + n // TG, 1), :, n % TG, :].rearrange("t p n -> p (t n)")

            def load_x(b, n):
                sp.dma_start(xr[n % 4][:], token_group("x", b, n)).then_inc(xr_in[n % 4], 16)

            def store_x1(b, n):
                sp.dma_start(token_group("x1", b, n), xr[n % 4][:]).then_inc(x1_out[n % 4], 16)

            def load_gate(b):
                sp.dma_start(gate[:], dram["gates"][0, bass.ds(b, 1)].rearrange("b k n -> (b k n)")
                             .partition_broadcast(P)).then_inc(gate_in, 16)

            def window(b, last):
                wait(bg_lo, b * NSP + R32)
                load_gate(b)
                for n in range(4):
                    load_x(b, n)
                if not last:
                    for u in range(NT):
                        sp.dma_start(xt[u][:], dram["x"][bass.ds(b * NT + (2 * NT + u), 1)]
                                     .rearrange("t p g n -> p (t g) n")).then_inc(x_in[u], 16)
                for h in range(H):
                    if h + NST - 1 < H or not last:
                        wait(st_full, b * (16 * H) + 16 * h + 1)
                        if h + NST - 1 == H:
                            wait(bg_lo, b * NSP + sp_at["qk", KC, 1] + 1 + R32)
                        load_stacks(h + NST - 1)
                    if h == 1:
                        wait(pv_done, b * (8 * H) + RING)
                        sp.dma_start(v_all[:, 12:16], v_last[:]).then_inc(v_in, 16)
                    for n in {1: (0, 1, 2), 2: (3,)}.get(h, ()):
                        wait(x1_ready, b * 8 + n + 1)
                        store_x1(b, n)
                        wait(x1_out[n], b * 32 + 16)
                        load_x(b, n + 4)
                    if h == 3:
                        for n in range(4, 8):
                            wait(x1_ready, b * 8 + n + 1)
                            store_x1(b, n)
                    if h == 4:
                        for n in range(4):
                            wait(x1_out[n], b * 32 + 32)
                        if last:
                            load_gate(NB)
                            for n in range(4):
                                load_x(NB, n)

            sp.wait_ge(r_lo, R_END)
            for h in range(NST - 1):
                load_stacks(h)
            with sp.Fori(0, NB - 1) as b:
                window(b, False)
            window(NB - 1, True)
            for n in range(8):
                sp.wait_ge(x1_ready, NB * 8 + n + 1)
                store_x1(NB, n)
                if n < 4:
                    sp.wait_ge(x1_out[n], 32 * NB + 16)
                    load_x(NB, n + 4)
            for n in range(4):
                sp.wait_ge(x1_out[n], 32 * NB + 32)

        @block.tensor
        def _(pe):
            wa = (t["wa_hi"], t["wa_lo"])
            hh = (h_hi, h_lo)
            SPLIT = ((0, 0), (0, 1), (1, 0))

            def transpose_chunk(out, rows, fc):
                for g in range(TG):
                    mm = nc.tensor.transpose(out[:, g * P:(g + 1) * P], rows(g)[:, fc * P:(fc + 1) * P], t["ident"][:])
                return mm

            def cols_product(out, c, u, chunks):
                for kc in chunks:
                    for k, (a, w) in enumerate(SPLIT):
                        mm = nc.tensor.matmul(out, wa[w][:, U_QKV + c // KC, kc, c % KC * P:(c % KC + 1) * P],
                                              hh[a][u][:, kc, :], start=(kc == 0 and k == 0),
                                              stop=(kc == KC - 1 and k == 2))
                return mm

            def rows_product(out, n, unit, cols, chunks):
                u, g = divmod(n, TG)
                for kc in chunks:
                    for k, (a, w) in enumerate(SPLIT):
                        mm = nc.tensor.matmul(out, hh[a][u][:, kc, g * P:(g + 1) * P], wa[w][:, unit, kc, cols],
                                              start=(kc == 0 and k == 0), stop=(kc == KC - 1 and k == 2))
                return mm

            def dense_piece(b, h, r):
                task, part, parts = dense[h, r]
                kind, n = task[0], bg_at[task]
                out = bg[n % 2]
                if part == 0:
                    before = order[n - 2] if n >= 2 else None
                    if before and before[0] == "p":
                        pe.wait_ge(gated_done, b * 8 + before[1] + 1)
                    elif before:
                        pe.wait_ge(bg_hi, b * NSP + sp_at[before] + 3)
                    else:
                        pe.wait_ge(bg_hi, b * NSP + n + 1)
                if kind == "o":
                    if task[2] == 0:
                        pe.wait_ge(o_ready, b * (2 * H) + 2 * H - 1 + task[1])
                    mm = transpose_chunk(out[:], lambda g: o_rows[:, TG * task[1] + g, :], task[2])
                elif kind == "x":
                    if task[2] == 0:
                        pe.wait_ge(x_ready, b * 8 + 8 + 4 * (task[1] + 1))
                    mm = transpose_chunk(out[:], lambda g: xt[task[1]][:, g, :], task[2])
                elif kind == "p":
                    if task[1] % TG == 0 and part == 0:
                        pe.wait_ge(bg_lo, b * NSP + sp_at["o", task[1] // TG, 3] + 1 + R32)
                    mm = rows_product(out[:], task[1], U_PROJ, slice(0, D), range(2 * part, 2 * part + 2))
                elif kind == "qk":
                    if part == 0 and task[1] == 0:
                        pe.wait_ge(bg_lo, b * NSP + sp_at["x", task[2], 3] + 1 + R32)
                    mm = cols_product(out[:], task[1], task[2], range(2 * part, 2 * part + 2))
                else:
                    mm = rows_product(out[:, 256 * part:256 * part + 256], 2 * task[2] + part, U_QKV + 2,
                                      slice(256 * task[1], 256 * task[1] + 256), range(KC))
                if part == parts - 1:
                    mm.then_inc(bg_full, 1)

            def scores_for_max(b, h, s):
                q, k = q_st[h % NST], k_st[h % NST]
                i, j = divmod(s, 2)
                if s == 0:
                    pe.wait_ge(stack_in[h % NST], b * (16 * HEAD_DMAS * HEADS_OF_SLOT) + 16 * HEAD_DMAS * (h // NST + 1))
                if s in (1, 2):
                    pe.wait_ge(mrow_done, b * (2 * H) + 2 * h + s)
                else:
                    pe.wait_ge(sm_free, b * (SM_HALVES * H) + SM_HALVES * h + max(s - 2, 0) + 1)
                nc.tensor.matmul(s_max[s % 3][:], q[0:STACK, i * P:(i + 1) * P], k[0:STACK, j * TILE:(j + 1) * TILE],
                                 start=True, stop=True).then_inc(sm_full, 1)

            def row_of_maxima(b, h):
                e = h % 2
                pe.wait_ge(max_done, b * H + h + 1)
                for u in range(NT):
                    for g in range(TG):
                        i = TG * u + g
                        mm = nc.tensor.matmul(s_max[(SM_HALVES + u) % 3][STACK:STACK + 1, g * P:(g + 1) * P],
                                              neg_max[:, e, i:i + 1], t["ident16"][:], start=True, stop=True)
                    mm.then_inc(mrow_full, 1)

            def scores_for_exp(b, h, i):
                half, kc = i // 8, i % 8
                if kc == 0:
                    pe.wait_ge(mrow_done, b * (2 * H) + 2 * h + half + 3)
                pe.wait_ge(exp_done, b * (16 * H) + 16 * h + i + 1)
                nc.tensor.matmul(s_exp[i % 2][:], k_st[h % NST][0:STACK + 1, kc * P:(kc + 1) * P],
                                 q_st[h % NST][0:STACK + 1, half * TILE:(half + 1) * TILE],
                                 start=True, stop=True).then_inc(st_full, 1)

            def use_pair(b, h, r):
                if r in DVE_PAIRS:
                    pe.wait_ge(lo_dve, b * (NDV * H) + NDV * h + DVE_PAIRS.index(r) + 1)
                else:
                    pe.wait_ge(lo_pool, b * (NPL * H) + NPL * h + POOL_PAIRS.index(r) + 1)
                if r % 4 == 0:
                    pe.wait_ge(raw_done, b * (2 * H) + 2 * h + r // 4 + 1)
                if r == 0 and h == 12:
                    pe.wait_ge(v_in, b * 16 + 16)
                hi = p32[r % RING][:].rearrange("p c n -> p (c n)").bitcast(BF16)
                for c in range(2):
                    kc = r % 4 * 2 + c
                    for g in range(TG):
                        at = c * TILE + g * P
                        nc.tensor.matmul(pv[:, g, 0:VW], hi[:, 2 * at + 1:2 * (at + P):2], v_all[:, h, kc, 0:VW],
                                         start=(r % 4 == 0 and c == 0 and g == 0), stop=False, skip_group_check=True)
                        mm = nc.tensor.matmul(pv[:, g, HD:VW], p_lo[r % RING][:, c, g * P:(g + 1) * P],
                                              v_all[:, h, kc, HD:VW], start=False,
                                              stop=(r % 4 == 3 and c == 1), skip_group_check=True)
                mm.then_inc(pv_done, 1)

            def window(b, last):
                for h in range(H):
                    for r in range(8):
                        sm = SM_AT[r] if h + 1 < H or not last else ()
                        for s in sm[0:1]:
                            scores_for_max(b, h + 1, s)
                        scores_for_exp(b, h, 2 * r)
                        scores_for_exp(b, h, 2 * r + 1)
                        for s in sm[1:2]:
                            scores_for_max(b, h + 1, s)
                        if r >= LAG:
                            use_pair(b, h, r - LAG)
                        elif h:
                            use_pair(b, h - 1, r - LAG + 8)
                        for s in sm[2:]:
                            scores_for_max(b, h + 1, s)
                        if r == ROW_AT and (h + 1 < H or not last):
                            row_of_maxima(b, h + 1)
                        if (h, r) in dense and not (last and h >= 4):
                            dense_piece(b, h, r)
                for r in range(8 - LAG, 8):
                    use_pair(b, H - 1, r)

            pe.wait_ge(consts, 2)
            for u in range(NT):
                pe.wait_ge(x_ready, 4 * (u + 1))
                for fc in range(KC):
                    if fc >= 2:
                        pe.wait_ge(r_hi, R_TILE * u + fc - 1)
                    transpose_chunk(s_exp[fc % 2][:], lambda g: xt[u][:, g, :], fc).then_inc(tp_full, 1)
                pe.wait_ge(r_lo, R_TILE * u + KC)
                for c in range(3 * KC):
                    if c >= 4:
                        pe.wait_ge(r_hi, R_TILE * u + c + 1)
                    elif u:
                        pe.wait_ge(r_hi, R_TILE * u - 4 + c + 1)
                    if c < 2 * KC:
                        mm = cols_product(work(c % 4), c, u, range(KC))
                    else:
                        half, j = divmod(c - 2 * KC, 2)
                        for k in range(2):
                            mm = rows_product(work(c % 4)[:, 256 * k:256 * k + 256], TG * u + 2 * j + k, U_QKV + 2,
                                              slice(256 * half, 256 * half + 256), range(KC))
                    mm.then_inc(wk_full, 1)
            pe.wait_ge(r_hi, R_END)
            for s in range(SM_HALVES):
                scores_for_max(0, 0, s)
            row_of_maxima(0, 0)
            pe.wait_ge(k_rows, NST)
            with pe.Fori(0, NB - 1) as b:
                window(b, False)
            window(NB - 1, True)
            for u in range(NT):
                pe.wait_ge(o_ready, NB * 2 * H + 2 * H - 1 + u)
                for fc in range(KC):
                    if u or fc >= 2:
                        pe.wait_ge(r_hi, R_END + KC * u + fc - 1)
                    transpose_chunk(s_exp[fc % 2][:], lambda g: o_rows[:, TG * u + g, :], fc).then_inc(tp_full, 1)
                pe.wait_ge(r_lo, R_END + KC * (u + 1))
                for g in range(TG):
                    if u:
                        pe.wait_ge(wk_free, g + 1)
                    rows_product(work(g), TG * u + g, U_PROJ, slice(0, D), range(KC)).then_inc(wk_full, 1)

        @block.scalar
        def _(act):
            def for_split(n, done, src, places, **func):
                nc.scalar.activation(r32[n % R32][:], src, ACT.Identity, **func)
                for piece, place in places:
                    ins = nc.scalar.activation(place, piece, ACT.Identity, **func)
                ins.then_inc(done, 1)

            def norm_vectors(batch):
                for k, ab in enumerate((t["ln_a"], t["ln_b"])):
                    nc.scalar.copy(ln_ab[:, k, :], ab[:, 0, :, bass.ds(batch, 1)]).then_inc(ab_ready, 1)

            def norm_args(fc):
                return dict(scale=ln_ab[:, 0, fc:fc + 1], bias=ln_ab[:, 1, fc:fc + 1])

            def qk_args(c):
                return dict(bias=t["cols"][:, C_QK + c:C_QK + c + 1])

            def v_hi(src, half, j):
                return [(by_heads(src)[:, :, heads], place) for heads, place in v_places(half, j, False)]

            def empty_bg(b, task):
                kind, n, s = task[0], bg_at[task], sp_at[task]
                act.wait_ge(bg_full, b * NBG + n + 1)
                act.wait_ge(bg_lo, b * NSP + s + 1)
                src = bg[n % 2][:]
                if kind in ("o", "x"):
                    if kind == "x" and task[1:] == (0, 0):
                        act.wait_ge(ab_ready, b * 2 + 4)
                    for_split(s, bg_hi, src, [(src, h_hi[task[1]][:, task[2], :])],
                              **(norm_args(task[2]) if kind == "x" else {}))
                elif kind == "qk":
                    c, u = task[1:]
                    for_split(s, bg_hi, src, [(src, qk_hi[:, c, u * TILE:(u + 1) * TILE])], **qk_args(c))
                else:
                    for_split(s, bg_hi, src, v_hi(src, *task[1:]))

            def empty_pv(b, h, half):
                act.wait_ge(pv_done, b * (8 * H) + 8 * h + 4 * (half + 1) + RING)
                act.wait_ge(o_ready, b * (2 * H) + 2 * h + half + 2 * H - 1)
                nc.scalar.copy(raw[half][:], pv[:, :, 0:VW]).then_inc(raw_done, 1)

            def take_row(b, h):
                for u in range(NT):
                    act.wait_ge(mrow_full, b * (2 * H) + 2 * h + u + 1)
                    nc.scalar.copy(q_st[h % NST][STACK:STACK + 1, u * TILE:(u + 1) * TILE],
                                   s_max[(SM_HALVES + u) % 3][STACK:STACK + 1, :]).then_inc(mrow_done, 1)

            def window(b, last):
                if not last:
                    norm_vectors(b + 1)
                for h in range(H):
                    for r in range(8):
                        for i in (2 * r, 2 * r + 1):
                            act.wait_ge(st_full, b * (16 * H) + 16 * h + i + 2)
                            if i % 2 == 0:
                                act.wait_ge(pv_done, b * (8 * H) + 8 * h + r + 1)
                            nc.scalar.activation(p32[r % RING][:, i % 2, :], s_exp[i % 2][:], ACT.Exp,
                                                 scale=SCALE).then_inc(exp_done, 1)
                            if i % 2:
                                if r == LAG - 1 and h:
                                    empty_pv(b, h - 1, 1)
                                if r == LAG + 3:
                                    empty_pv(b, h, 0)
                                if r == ROW_AT and (h + 1 < H or not last):
                                    take_row(b, h + 1)
                                task = filled(h, r, 1)
                                if task and task[0] != "p" and (done_in_last(task) or not last):
                                    empty_bg(b, task)
                empty_pv(b, H - 1, 1)

            act.wait_ge(consts, 2)
            norm_vectors(0)
            act.wait_ge(ab_ready, 2)
            for u in range(NT):
                for n in range(R_TILE):
                    c = n - KC
                    if R_TILE * u + n >= R32:
                        act.wait_ge(r_lo, R_TILE * u + n - R32 + 1)
                    if c < 0:
                        act.wait_ge(tp_full, KC * u + n + 1)
                        src = s_exp[n % 2][:]
                        for_split(n, r_hi, src, [(src, h_hi[u][:, n, :])], **norm_args(n))
                    else:
                        act.wait_ge(wk_full, 3 * KC * u + c + 1)
                        src = work(c % 4)
                        if c < 2 * KC:
                            for_split(n, r_hi, src, [(src, qk_hi[:, c, u * TILE:(u + 1) * TILE])], **qk_args(c))
                        else:
                            half, j = divmod(c - 2 * KC, 2)
                            for_split(n, r_hi, src, v_hi(src, half, 2 * u + j))
            take_row(0, 0)
            act.wait_ge(r_lo, R_END)
            with act.Fori(0, NB - 1) as b:
                window(b, False)
            window(NB - 1, True)
            act.wait_ge(bg_lo, (NB - 1) * NSP + 2 * KC + R32)
            for u in range(NT):
                for fc in range(KC):
                    act.wait_ge(tp_full, NT * KC + KC * u + fc + 1)
                    if KC * u + fc >= R32:
                        act.wait_ge(r_lo, R_END + KC * u + fc - R32 + 1)
                    for_split(fc, r_hi, s_exp[fc % 2][:], [(s_exp[fc % 2][:], h_hi[u][:, fc, :])])

        @block.gpsimd
        def _(pool):
            def inverse_deviation(b, u):
                pool.wait_ge(var_done, b * NT + u + 1)
                nc.gpsimd.tensor_tensor(rstd[:, u, :], var_eps[:, u, :], t["minus_half"][:], ALU.pow).then_inc(rstd_done, 1)

            def add_bias(b, n):
                if n == 0:
                    pool.wait_ge(gate_in, b * 16 + 16)
                pool.wait_ge(xr_in[n % 4], b * 32 + 16 * (n // 4 + 1))
                nc.gpsimd.tensor_tensor(xr[n % 4][:], xr[n % 4][:], gate[:, 1, :], ALU.add).then_inc(x_biased, 1)

            bias_at = {(0, 2): 0, (0, 4): 1, (0, 6): 2, (1, 1): 3, (2, 1): 4, (2, 4): 5, (2, 6): 6, (3, 2): 7}

            def window(b, last):
                for h in range(H):
                    for r in POOL_PAIRS:
                        if (h, r) in bias_at:
                            add_bias(b, bias_at[h, r])
                        if h in (2, 3) and r == 1 and not last:
                            inverse_deviation(b + 1, h - 2)
                        pool.wait_ge(exp_done, b * (16 * H) + 16 * h + 2 * r + 4)
                        flat = p32[r % RING][:].rearrange("p c n -> p (c n)")
                        nc.gpsimd.tensor_tensor(p_lo[r % RING][:].rearrange("p c n -> p (c n)"), flat,
                                                flat.bitcast(BF16)[:, 1::2], ALU.subtract).then_inc(lo_pool, 1)

            nc.gpsimd.memset(v_all[:, :, :, VW - 1], 1.0).then_inc(consts, 1)
            nc.gpsimd.memset(v_last[:], 1.0).then_inc(consts, 1)
            nc.gpsimd.memset(o_rows[:], 0.0).then_inc(o_ready, 2 * H)
            for u in range(NT):
                inverse_deviation(0, u)
            pool.wait_ge(rstd_done, NT)
            for e in range(NST):
                nc.gpsimd.memset(k_st[e][STACK:STACK + 1, :], M_UNIT).then_inc(k_rows, 1)
                pool.wait_ge(k_rows, e + 1)
            with pool.Fori(0, NB - 1) as b:
                window(b, False)
            window(NB - 1, True)
            for n in range(GPB):
                add_bias(NB, n)

        @block.vector
        def _(dve):
            def statistics(b, u, groups):
                if groups[0] == 0 and not isinstance(b, int):
                    dve.wait_ge(x_in[u], b * 16)
                for g in groups:
                    nc.vector.bn_stats(stats[:, u, g, :], xt[u][:, g, :]).then_inc(bn_done, 1)
                if groups[-1] == TG - 1:
                    dve.wait_ge(bn_done, b * 8 + 4 * u + 4)
                    nc.vector.memset(waited[:], 0.0)
                    for g in range(TG):
                        nc.vector.bn_aggr(mv[:, u, g, :], stats[:, u, g, :]).then_inc(agg_done, 1)
                    dve.wait_ge(agg_done, b * 8 + 4 * u + 4)
                    nc.vector.tensor_scalar(var_eps[:, u, :], mv[:, u, :, 1], 1e-5, None, ALU.add).then_inc(var_done, 1)

            def normalise_x(b, u, groups):
                if groups[0] == 0:
                    dve.wait_ge(rstd_done, b * NT + u + 1)
                for g in groups:
                    nc.vector.tensor_scalar(xt[u][:, g, :], xt[u][:, g, :], mv[:, u, g, 0:1], rstd[:, u, g:g + 1],
                                            ALU.subtract, ALU.mult).then_inc(x_ready, 1)

            def low_of(n, done, places):
                for piece, hi, lo in places(r32[n % R32][:]):
                    ins = nc.vector.tensor_tensor(lo, piece, hi, ALU.subtract)
                ins.then_inc(done, 1)

            def norm_low(u, fc):
                return lambda x: [(x, h_hi[u][:, fc, :], h_lo[u][:, fc, :])]

            def qk_low(c, u):
                tok = slice(u * TILE, (u + 1) * TILE)
                return lambda x: [(x, qk_hi[:, c, tok], qk_lo[:, c, tok])]

            def v_low(half, j):
                return lambda x: [(by_heads(x)[:, :, heads], hi, lo) for (heads, hi), (_, lo) in
                                  zip(v_places(half, j, False), v_places(half, j, True))]

            def split_bg(b, task):
                dve.wait_ge(bg_hi, b * NSP + sp_at[task] + 3)
                low_of(sp_at[task], bg_lo, {"o": norm_low, "x": norm_low, "qk": qk_low, "v": v_low}[task[0]](*task[1:]))

            def residual(b, n, product, full, value, free, free_value):
                dve.wait_ge(full, value)
                nc.vector.tensor_tensor(gated[n % 2][:], product, gate[:, 0, :], ALU.mult).then_inc(free, 1)
                dve.wait_ge(free, free_value)
                dve.wait_ge(x_biased, b * 8 + n + 1)
                nc.vector.tensor_tensor(xr[n % 4][:], gated[n % 2][:], xr[n % 4][:], ALU.add).then_inc(x1_ready, 1)

            def take_max(b, h, s):
                e = h % 2
                dve.wait_ge(sm_full, b * (SM_HALVES * H) + SM_HALVES * h + s + 1)
                nc.vector.reduce_max(half_max[:, e, s // 2, s % 2:s % 2 + 1], s_max[s % 3][:], AX_X).then_inc(sm_free, 1)
                if s == SM_HALVES - 1:
                    dve.wait_ge(sm_free, b * (SM_HALVES * H) + SM_HALVES * h + SM_HALVES + 1)
                    nc.vector.tensor_tensor(row_max[:, e, :], half_max[:, e, :, 0], half_max[:, e, :, 1],
                                            ALU.max).then_inc(both_done, 1)
                    dve.wait_ge(both_done, b * H + h + 1)
                    nc.vector.tensor_scalar(neg_max[:, e, :], row_max[:, e, :], -1.0 / M_UNIT, None,
                                            ALU.mult).then_inc(max_done, 1)

            def low_part(b, h, r):
                dve.wait_ge(exp_done, b * (16 * H) + 16 * h + 2 * r + 4)
                flat = p32[r % RING][:].rearrange("p c n -> p (c n)")
                nc.vector.tensor_tensor(p_lo[r % RING][:].rearrange("p c n -> p (c n)"), flat,
                                        flat.bitcast(BF16)[:, 1::2], ALU.subtract).then_inc(lo_dve, 1)

            def normalise(b, h, half):
                n = 2 * h + half
                dve.wait_ge(raw_done, b * (2 * H) + n + 2)
                nc.vector.reciprocal(inv_l[half][:], raw[half][:, :, VW - 1]).then_inc(inv_done, 1)
                nc.vector.tensor_tensor(o_sum[half][:], raw[half][:, :, HD:2 * HD], raw[half][:, :, 0:HD],
                                        ALU.add).then_inc(sum_done, 1)
                if n == 0:
                    dve.wait_ge(bg_full, b * NBG + bg_at["o", NT - 1, KC - 1] + 1)
                dve.wait_ge(inv_done, b * (2 * H) + n + 1)
                dve.wait_ge(sum_done, b * (2 * H) + n + 1)
                nc.vector.tensor_tensor(o_rows[:, TG * half:TG * (half + 1), h * HD:(h + 1) * HD], o_sum[half][:],
                                        inv_l[half][:].unsqueeze(2).to_broadcast([P, TG, HD]),
                                        ALU.mult).then_inc(o_ready, 1)

            def window(b, last):
                for h in range(H):
                    for r in range(8):
                        if h + 1 < H or not last:
                            for s in SM_AT[r]:
                                take_max(b, h + 1, s)
                        if r == 0 and h:
                            low_part(b, h - 1, 7)
                        if r == 4:
                            low_part(b, h, 3)
                        if r == 7:
                            if h:
                                normalise(b, h - 1, 1)
                            normalise(b, h, 0)
                        task = filled(h, r, 1)
                        if task and task[0] == "p":
                            n, k = task[1], bg_at[task]
                            residual(b, n, bg[k % 2][:], bg_full, b * NBG + k + 1, gated_done, b * 8 + n + 1)
                        task = filled(h, r, 2)
                        if task and task[0] != "p" and (done_in_last(task) or not last):
                            split_bg(b, task)
                        if not last:
                            if h in (1, 2) and r in (2, 3, 6, 7):
                                g = (2, 3, 6, 7).index(r)
                                statistics(b + 1, h - 1, [g])
                            if (3, 4) <= (h, r) < (4, 4):
                                normalise_x(b + 1, h - 3, [r % TG])
                low_part(b, H - 1, 7)
                normalise(b, H - 1, 1)

            for i in range(2):
                nc.vector.memset(inv_l[0][:, i:i + 1], 0.0).then_inc(exp_done, 1)
            nc.vector.memset(t["minus_half"][:], -0.5).then_inc(bg_lo, R32)
            nc.vector.memset(row_max[:], 0.0).then_inc(sm_free, 1)
            nc.vector.memset(neg_max[:], 0.0).then_inc(mrow_done, 2)
            nc.vector.memset(inv_l[0][:, 2:3], 0.0).then_inc(st_full, 1)
            nc.vector.memset(inv_l[0][:, 3:4], 0.0).then_inc(raw_done, 1)
            nc.vector.memset(waited[:], 0.0).then_inc(bg_hi, 2)
            for i in range(RING):
                nc.vector.memset(inv_l[1][:, i:i + 1], 0.0).then_inc(pv_done, 1)
            for u in range(NT):
                statistics(0, u, range(TG))
                normalise_x(0, u, range(TG))
            for u in range(NT):
                for n in range(R_TILE):
                    c = n - KC
                    dve.wait_ge(r_hi, R_TILE * u + n + 1)
                    if c < 0:
                        low_of(n, r_lo, norm_low(u, n))
                    elif c < 2 * KC:
                        low_of(n, r_lo, qk_low(c, u))
                    else:
                        half, j = divmod(c - 2 * KC, 2)
                        low_of(n, r_lo, v_low(half, 2 * u + j))
            for s in range(SM_HALVES):
                take_max(0, 0, s)
            with dve.Fori(0, NB - 1) as b:
                window(b, False)
            window(NB - 1, True)
            for u in range(NT):
                for fc in range(KC):
                    dve.wait_ge(r_hi, R_END + KC * u + fc + 1)
                    low_of(fc, r_lo, norm_low(u, fc))
                for g in range(TG):
                    n = TG * u + g
                    residual(NB, n, work(g), wk_full, NT * 3 * KC + n + 1, wk_free, n + 1)


def feed_forward(nc, ctx, t, dram):
    def sb(name, shape, dt):
        return ctx.enter_context(nc.sbuf_tensor(name, shape, dt))

    def sem(name):
        return ctx.enter_context(nc.semaphore(name))

    xt = [sb(f"fx{u}", [P, TG, D], F32) for u in range(NT)]
    xn = sb("xn", [P, TG, D], F32)
    stats = sb("fstats", [P, TG, 6], F32)
    mv = sb("fmv", [P, TG, 2], F32)
    var_eps = sb("fvar_eps", [P, TG], F32)
    rstd = sb("frstd", [P, TG], F32)
    h_hi = [sb(f"fh_hi{u}", [P, KC, TILE], F16) for u in range(NT)]
    h_lo = [sb(f"fh_lo{u}", [P, KC, TILE], BF16) for u in range(NT)]
    r32 = [sb(f"fr32_{i}", [P, TILE], F32) for i in range(4)]
    a_hi = [sb(f"a_hi{i}", [P, TILE], F16) for i in range(4)]
    a_lo = [sb(f"a_lo{i}", [P, TILE], BF16) for i in range(4)]
    gate_rows = sb("fgates", [P, 3, 2, D], F32)
    gate = [gate_rows[:, s] for s in range(3)]
    gated = [sb(f"fgated{i}", [P, D], F32) for i in range(2)]
    waited = sb("fwaited", [P, 1], F32)
    mask_b = sb("mask_b", [P, GPB], F32)
    ln_ab = sb("ln_ab", [P, 2, 4, KC], F32)
    gb_masked = sb("gb_masked", [P, D], F32)
    stage = dict(gates=gate_rows[:, 1:3].rearrange("p s k n -> p (s k n)"),
                 tile=xt[1][:].rearrange("p g n -> p (g n)"), xn=xn[:].rearrange("p g n -> p (g n)"))
    stage_of = ["gates", "tile"] + ["xn", "gates"] * 5 + ["gates"] * 4
    turn_of = [stage_of[:n].count(stage_of[n]) for n in range(N_FF_UNITS)]
    unit_at = {(0, m): m + 1 for m in range(1, 11)}
    unit_at.update({(0, 12): 12, (0, 14): 13, (1, 1): 14, (1, 3): 15})

    tp = [ctx.enter_context(nc.psum_tensor(f"tp{i}", [P, TILE], F32)) for i in range(2)]
    hid = [ctx.enter_context(nc.psum_tensor(f"hid{i}", [P, TILE], F32)) for i in range(2)]
    acc = [ctx.enter_context(nc.psum_tensor(f"acc{g}", [P, D], F32)) for g in range(TG)]

    NCALL = 3 * NT
    site_of = [c // NT for c in range(NCALL)]
    chunks = [SITES[s]["chunks"] for s in site_of]
    before = [sum(chunks[:c]) for c in range(NCALL)]
    PER_BATCH = sum(chunks)
    assert all(m % 4 == 0 for m in chunks)
    unit_order = [s[k] + i for s in SITES for i in range(s["chunks"] // KC) for k in ("up", "down")]
    assert sorted(unit_order) == list(range(N_FF_UNITS))
    ENTRIES = PER_BATCH + 4 * NCALL

    def hidden_entry(c, m):
        return 4 + before[c] + 4 * c + (m if m < chunks[c] - 1 else m + 2)

    def norm_entry(c, fc):
        return fc if c == 0 else 4 + before[c - 1] + 4 * (c - 1) + chunks[c - 1] - 1 + (fc if fc < 2 else fc + 1)

    x_in = [sem(f"fx_in{u}") for u in range(NT)]
    gate_in = [sem(f"fgate_in{s}") for s in range(3)]
    bn_done = sem("fbn_done")
    agg_done = sem("fagg_done")
    var_done = sem("fvar_done")
    rstd_done = sem("frstd_done")
    xn_ready = sem("xn_ready")
    tp_full = sem("ftp_full")
    hid_full = sem("hid_full")
    r32_full = sem("fr32_full")
    split_hi = sem("fsplit_hi")
    split_done = sem("fsplit_done")
    down_done = sem("down_done")
    acc_full = sem("acc_full")
    acc_free = sem("acc_free")
    x_biased = sem("fx_biased")
    mask_ready = sem("mask_ready")
    gb_done = sem("gb_done")
    x_new = sem("x_new")
    out_done = [sem(f"out_done{u}") for u in range(NT)]
    sp_turn = sem("fsp_turn")
    act_turn = sem("act_turn")
    abc_ready = sem("abc_ready")
    consts = sem("fconsts")
    stage_in = {k: sem(f"wstage_in_{k}") for k in stage}
    w_hi = sem("w_hi")
    w_lo = sem("w_lo")
    copied = sem("x1_copied")

    with nc.Block() as block:

        @block.sync
        def _(sp):
            def wait(sem_, value):
                sp.wait_ge(sem_, value if isinstance(value, int) else sp.snap(value))
                sp.sem_inc(sp_turn, 1)

            def load(u, tile):
                sp.dma_start(xt[u][:], dram["x1"][bass.ds(tile + NT, 1)].rearrange("t p g n -> p (t g) n")).then_inc(x_in[u], 16)

            def batch(b):
                for s in range(3):
                    if s == 2:
                        wait(x_new, b * 24 + 20)
                        sp.dma_start(dram["out"][bass.ds(b * NT, 1)].rearrange("t p g n -> p (t g) n"), xt[0][:]).then_inc(out_done[0], 16)
                        wait(out_done[0], b * 16 + 16)
                        load(0, b * NT + NT)
                    wait(x_new, b * 24 + 8 * s + 8)
                    sp.dma_start(gate[s], dram["gates"][1 + s, bass.ds(b + 1, 1)].rearrange("b k n -> (b k n)").partition_broadcast(P)).then_inc(gate_in[s], 16)
                sp.dma_start(dram["out"][bass.ds(b * NT + 1, 1)].rearrange("t p g n -> p (t g) n"), xt[1][:]).then_inc(out_done[1], 16)
                wait(out_done[1], b * 16 + 16)
                load(1, b * NT + NT + 1)

            def load_unit(n):
                if turn_of[n]:
                    sp.wait_ge(w_lo, max(k for k in range(n) if stage_of[k] == stage_of[n]) + 1)
                elif stage_of[n] == "xn":
                    sp.wait_ge(tp_full, KC)
                sp.dma_start(stage[stage_of[n]], dram["w"][N_ATT_UNITS + unit_order[n]]).then_inc(stage_in[stage_of[n]], 16)

            sp.dma_start(xt[0][:], dram["x1"][NT]).then_inc(x_in[0], 16)
            for n in range(2):
                load_unit(n)
            sp.dma_start(gate[0], dram["gates"][1, 0:1].rearrange("b k n -> (b k n)").partition_broadcast(P)).then_inc(gate_in[0], 16)
            load_unit(2)
            sp.wait_ge(w_lo, 2)
            sp.dma_start(xt[1][:], dram["x1"][NT + 1]).then_inc(x_in[1], 16)
            for n in range(3, N_FF_UNITS):
                load_unit(n)
            sp.wait_ge(w_lo, N_FF_UNITS)
            for s in range(1, 3):
                sp.dma_start(gate[s], dram["gates"][1 + s, 0:1].rearrange("b k n -> (b k n)").partition_broadcast(P)).then_inc(gate_in[s], 16)
            sp.dma_start(dram["x1"][(NB + 1) * NT:(NB + 2) * NT], dram["x1"][0:NT]).then_inc(copied, 16)
            sp.wait_ge(copied, 16)
            batch(0)
            with sp.Fori(1, NB) as b:
                batch(b)
            for u in range(NT):
                sp.wait_ge(x_in[u], 16 * (NB + 1))
            for s in range(3):
                sp.wait_ge(gate_in[s], 16 * (NB + 1))

        @block.tensor
        def _(pe):
            wf = (t["wf_hi"], t["wf_lo"])

            def transpose_chunk(b, c, fc):
                if fc == 0:
                    pe.wait_ge(xn_ready, b * 24 + 4 * c + 4)
                if fc >= 2:
                    pe.wait_ge(r32_full, b * ENTRIES + norm_entry(c, fc - 2) + 1)
                for g in range(TG):
                    mm = nc.tensor.transpose(tp[fc % 2][:, g * P:(g + 1) * P], xn[:, g, fc * P:(fc + 1) * P], t["ident"][:])
                mm.then_inc(tp_full, 1)

            def first_use(b, c, m):
                return isinstance(b, int) and c % NT == 0 and m % KC == 0

            def up(b, c, m):
                u, un, col = c % NT, SITES[site_of[c]]["up"] + m // KC, m % KC * P
                if first_use(b, c, m):
                    pe.wait_ge(w_lo, unit_order.index(un) + 1)
                if m == 0:
                    pe.wait_ge(split_done, b * ENTRIES + norm_entry(c, 3) + 1)
                if m >= 2:
                    pe.wait_ge(r32_full, b * ENTRIES + hidden_entry(c, m - 2) + 1)
                elif c:
                    pe.wait_ge(r32_full, b * ENTRIES + hidden_entry(c - 1, chunks[c - 1] - 2 + m) + 1)
                for kc in range(KC):
                    for k, (w, a) in enumerate(((wf[0], h_hi), (wf[0], h_lo), (wf[1], h_hi))):
                        mm = nc.tensor.matmul(hid[m % 2][:], w[:, un, kc, col:col + P], a[u][:, kc, :],
                                              start=(kc == 0 and k == 0), stop=(kc == KC - 1 and k == 2))
                mm.then_inc(hid_full, 1)

            def down(b, c, m):
                un, kc = SITES[site_of[c]]["down"] + m // KC, m % KC
                if first_use(b, c, m):
                    pe.wait_ge(w_lo, unit_order.index(un) + 1)
                pe.wait_ge(split_done, b * ENTRIES + hidden_entry(c, m) + 1)
                last = m == chunks[c] - 1
                for g in range(TG):
                    if m == 0:
                        pe.wait_ge(acc_free, b * 24 + 4 * c + g + 1)
                    for k, (a, w) in enumerate(((a_hi, wf[0]), (a_hi, wf[1]), (a_lo, wf[0]))):
                        mm = nc.tensor.matmul(acc[g][:], a[m % 4][:, g * P:(g + 1) * P], w[:, un, kc, :],
                                              start=(m == 0 and k == 0), stop=(last and k == 2))
                    if last and g < TG - 1:
                        mm.then_inc(acc_full, 1)
                mm.then_inc(down_done, 1)

            def batch(b):
                for c in range(NCALL):
                    n = chunks[c]
                    for m in range(n):
                        up(b, c, m)
                        if m == n - 1:
                            transpose_chunk(b, c + 1, 2)
                            transpose_chunk(b, c + 1, 3)
                        if m >= 2:
                            down(b, c, m - 2)
                        if m == n - 2:
                            transpose_chunk(b, c + 1, 0)
                            transpose_chunk(b, c + 1, 1)
                    down(b, c, n - 2)
                    down(b, c, n - 1)

            pe.wait_ge(consts, 1)
            for fc in range(KC):
                transpose_chunk(0, 0, fc)
            batch(0)
            with pe.Fori(1, NB) as b:
                batch(b)

        @block.scalar
        def _(act):
            def entry(b, n, src, func, bias, scale=1.0):
                if not isinstance(n, int) or n >= 4 or not isinstance(b, int):
                    act.wait_ge(split_done, b * ENTRIES + n - 3)
                nc.scalar.activation(r32[n % 4][:], src, func, bias=bias, scale=scale).then_inc(r32_full, 1)

            def high_of_unit(n):
                act.wait_ge(stage_in[stage_of[n]], 16 * (turn_of[n] + 1))
                nc.scalar.copy(t["wf_hi"][:, unit_order[n]].rearrange("p k n -> p (k n)"), stage[stage_of[n]]).then_inc(w_hi, 1)

            def norm_chunk(b, c, fc):
                k = site_of[c] if c < NCALL else 3
                act.wait_ge(tp_full, b * 24 + 4 * c + fc + 1)
                entry(b, norm_entry(c, fc), tp[fc % 2][:], ACT.Identity, ln_ab[:, 1, k, fc:fc + 1],
                      ln_ab[:, 0, k, fc:fc + 1])

            def batch(b):
                act.wait_ge(r32_full, b * ENTRIES + 4)
                act.sem_inc(act_turn, 1)
                for k, ab in enumerate((t["ln_a"], t["ln_b"])):
                    nc.scalar.copy(ln_ab[:, k, 0:3, :], ab[:, 1:4, :, bass.ds(b, 1)]).then_inc(abc_ready, 1)
                    nc.scalar.copy(ln_ab[:, k, 3, :], ab[:, 1, :, bass.ds(b + 1, 1)]).then_inc(abc_ready, 1)
                act.wait_ge(abc_ready, b * 4 + 8)
                for c in range(NCALL):
                    n, s = chunks[c], SITES[site_of[c]]
                    for m in range(n):
                        if m == n - 1:
                            norm_chunk(b, c + 1, 0)
                            norm_chunk(b, c + 1, 1)
                        col = C_UP + s["bias"] + m
                        act.wait_ge(hid_full, b * PER_BATCH + before[c] + m + 1)
                        entry(b, hidden_entry(c, m), hid[m % 2][:], s["act"], t["cols"][:, col:col + 1])
                        if isinstance(b, int) and (c, m) in unit_at:
                            high_of_unit(unit_at[c, m])
                    norm_chunk(b, c + 1, 2)
                    norm_chunk(b, c + 1, 3)

            act.wait_ge(consts, 1)
            for k, ab in enumerate((t["ln_a"], t["ln_b"])):
                nc.scalar.copy(ln_ab[:, k, 0, :], ab[:, 1, :, 0]).then_inc(abc_ready, 2)
            act.wait_ge(abc_ready, 4)
            high_of_unit(0)
            for fc in range(KC):
                norm_chunk(0, 0, fc)
            high_of_unit(1)
            batch(0)
            with act.Fori(1, NB) as b:
                batch(b)

        @block.gpsimd
        def _(pool):
            def inverse_deviation(n):
                pool.wait_ge(var_done, n + 1)
                nc.gpsimd.tensor_tensor(rstd[:], var_eps[:], t["minus_half"][:], ALU.pow).then_inc(rstd_done, 1)

            def batch(b):
                nc.gpsimd.tensor_copy(mask_b[:], t["mask"][:, bass.ds(b * GPB, GPB)]).then_inc(mask_ready, 1)
                pool.wait_ge(mask_ready, b + 1)
                for c in range(NCALL):
                    s, u = site_of[c], c % NT
                    pool.wait_ge(gate_in[s], b * 16 + 16)
                    pool.wait_ge(xn_ready, b * 24 + 4 * c + 4)
                    for g in range(TG):
                        gb = gate[s][:, 1, :]
                        if s == 1:
                            pool.wait_ge(x_biased, b * 24 + 4 * c + g)
                            nc.gpsimd.tensor_tensor(gb_masked[:], gb, mask_b[:, TG * u + g:TG * u + g + 1].to_broadcast([P, D]),
                                                    ALU.mult).then_inc(gb_done, 1)
                            pool.wait_ge(gb_done, b * 8 + 4 * u + g + 1)
                            gb = gb_masked[:]
                        nc.gpsimd.tensor_tensor(xt[u][:, g, :], xt[u][:, g, :], gb, ALU.add).then_inc(x_biased, 1)
                    inverse_deviation(b * NCALL + (c + 1))

            pool.wait_ge(consts, 1)
            inverse_deviation(0)
            batch(0)
            with pool.Fori(1, NB) as b:
                batch(b)

        @block.vector
        def _(dve):
            def split(b, n, hi, lo):
                dve.wait_ge(r32_full, b * ENTRIES + n + 1)
                nc.vector.tensor_copy(hi, r32[n % 4][:]).then_inc(split_hi, 1)
                dve.wait_ge(split_hi, b * ENTRIES + n + 1)
                nc.vector.tensor_tensor(lo, r32[n % 4][:], hi, ALU.subtract).then_inc(split_done, 1)

            def split_norm(b, c, fc):
                u = c % NT
                split(b, norm_entry(c, fc), h_hi[u][:, fc, :], h_lo[u][:, fc, :])

            def low_of_unit(n):
                dve.wait_ge(w_hi, n + 1)
                w = unit_order[n]
                nc.vector.tensor_tensor(t["wf_lo"][:, w].rearrange("p k n -> p (k n)"), stage[stage_of[n]],
                                        t["wf_hi"][:, w].rearrange("p k n -> p (k n)"), ALU.subtract).then_inc(w_lo, 1)

            def statistics(b, c, groups):
                u, n = c % NT, b * 24 + 4 * c
                eps = SITES[site_of[c] if c < NCALL else 0]["eps"]
                if groups[0] == 0 and c in (0, 1, NCALL):
                    dve.wait_ge(x_in[u], b * 16 + 16 * (1 + c // NCALL))
                elif groups[0] == 0:
                    dve.wait_ge(x_new, b * 24 + 4 * (c - NT) + 4)
                for g in groups:
                    nc.vector.bn_stats(stats[:, g, :], xt[u][:, g, :]).then_inc(bn_done, 1)
                if groups[-1] == TG - 1:
                    dve.wait_ge(bn_done, n + 4)
                    nc.vector.memset(waited[:], 0.0)
                    for g in range(TG):
                        nc.vector.bn_aggr(mv[:, g, :], stats[:, g, :]).then_inc(agg_done, 1)
                    dve.wait_ge(agg_done, n + 4)
                    nc.vector.tensor_scalar(var_eps[:], mv[:, :, 1], eps, None, ALU.add).then_inc(var_done, 1)

            def normalise(b, c):
                u = c % NT
                dve.wait_ge(rstd_done, b * NCALL + (c + 1))
                if not (isinstance(b, int) and c == 0):
                    dve.wait_ge(tp_full, b * 24 + 4 * c)
                for g in range(TG):
                    nc.vector.tensor_scalar(xn[:, g, :], xt[u][:, g, :], mv[:, g, 0:1], rstd[:, g:g + 1],
                                            ALU.subtract, ALU.mult).then_inc(xn_ready, 1)

            def residual(b, c):
                s, u = site_of[c], c % NT
                for g in range(TG):
                    k = b * 24 + 4 * c + g
                    if g < TG - 1:
                        dve.wait_ge(acc_full, b * 18 + 3 * c + g + 1)
                    else:
                        dve.wait_ge(down_done, b * PER_BATCH + before[c] + chunks[c] + 4)
                    if s == 1:
                        nc.vector.scalar_tensor_tensor(
                            out=gated[g % 2][:], in0=acc[g][:], scalar=mask_b[:, TG * u + g:TG * u + g + 1],
                            in1=gate[s][:, 0, :], op0=ALU.mult, op1=ALU.mult).then_inc(acc_free, 1)
                    else:
                        nc.vector.tensor_tensor(gated[g % 2][:], acc[g][:], gate[s][:, 0, :], ALU.mult).then_inc(acc_free, 1)
                    dve.wait_ge(acc_free, k + 1 + 4)
                    dve.wait_ge(x_biased, k + 1)
                    nc.vector.tensor_tensor(xt[u][:, g, :], gated[g % 2][:], xt[u][:, g, :], ALU.add).then_inc(x_new, 1)

            def batch(b):
                for c in range(NCALL):
                    n = chunks[c]
                    for m in range(n):
                        if m == n - 1:
                            split_norm(b, c + 1, 0)
                            split_norm(b, c + 1, 1)
                        dve.wait_ge(down_done, b * PER_BATCH + before[c] + m + 1)
                        split(b, hidden_entry(c, m), a_hi[m % 4][:], a_lo[m % 4][:])
                        if isinstance(b, int) and (c, m) in unit_at:
                            low_of_unit(unit_at[c, m])
                        if m == n - 5:
                            statistics(b, c + 1, range(0, 2))
                        if m == n - 4:
                            statistics(b, c + 1, range(2, TG))
                        if m == n - 3:
                            normalise(b, c + 1)
                    split_norm(b, c + 1, 2)
                    split_norm(b, c + 1, 3)
                    residual(b, c)

            for i in range(4):
                nc.vector.memset(gated[0][:, i:i + 1], 0.0).then_inc(down_done, 1)
            for i in range(4):
                nc.vector.memset(gated[0][:, 4 + i:5 + i], 0.0).then_inc(acc_free, 1)
            nc.vector.memset(gb_masked[:], 0.0).then_inc(consts, 1)
            statistics(0, 0, range(TG))
            normalise(0, 0)
            low_of_unit(0)
            for fc in range(KC):
                split_norm(0, 0, fc)
            low_of_unit(1)
            batch(0)
            with dve.Fori(1, NB) as b:
                batch(b)


def build(nc, dram):
    with ExitStack() as ctx:
        def sb(name, shape, dt, to=ctx):
            return to.enter_context(nc.sbuf_tensor(name, shape, dt))

        t = dict(
            cols=sb("cols", [P, NCOLS], F32),
            ident=sb("ident", [P, P], F32),
            ident16=sb("ident16", [P, P], F16),
            mask=sb("mask", [P, NB * GPB], F32),
            minus_half=sb("minus_half", [P, TG], F32),
            ln_a=sb("ln_a", [P, 4, KC, NB + 1], F32),
            ln_b=sb("ln_b", [P, 4, KC, NB + 1], F32),
        )
        with ExitStack() as att:
            t["xt"] = [sb(f"xt{u}", [P, TG, D], F32, att) for u in range(NT)]
            t["wa_hi"] = sb("wa_hi", [P, N_ATT_UNITS, KC, D], F16, att)
            t["wa_lo"] = sb("wa_lo", [P, N_ATT_UNITS, KC, D], BF16, att)
            with ExitStack() as s:
                prologue(nc, s, t, dram)
            with ExitStack() as s:
                attention(nc, s, t, dram)
        t["wf_hi"] = sb("wf_hi", [P, N_FF_UNITS, KC, D], F16)
        t["wf_lo"] = sb("wf_lo", [P, N_FF_UNITS, KC, D], BF16)
        with ExitStack() as s:
            feed_forward(nc, s, t, dram)


def kernel(**inputs):
    import concourse.bacc as bacc
    from concourse.bass_utils import run_bass_kernel_spmd as run

    a = {k: np.asarray(v) for k, v in inputs.items()}

    def units(w):
        r, c = w.shape[0] // D, w.shape[1] // D
        return w.reshape(r, KC, P, c, D).transpose(0, 3, 2, 1, 4).reshape(r * c, P, KC * D)

    def columns(v):
        return v.reshape(-1, P).T

    ada_b = [a["L0_cond_bt"][0:3 * D], a["L0_cond_bt"][3 * D:6 * D], a["L1_cond_ada_b"], a["L1_cond_ffada_b"]]
    arrays = {
        "x": np.concatenate([a["x"][0:1], a["x"]]),
        "condT": a["cond_1024"].reshape(NB, KC, P).transpose(2, 1, 0),
        "mask": np.ascontiguousarray(a["mask_BxS_bk0"].reshape(NB * GPB, P).T),
        "ident": np.eye(P, dtype=np.float32),
        "ada": np.concatenate([units(a["L0_cond_Wt"]), units(a["L1_cond_ada_w"]), units(a["L1_cond_ffada_w"])]),
        "w": np.concatenate([units(a[k]) for k in (
            "L0_cond_Wqkv", "L0_cond_Wproj", "L0_cond_W1", "L0_cond_W2", "L1_cond_ssm_w1", "L1_cond_bwd_w1",
            "L1_cond_ssm_w2", "L1_cond_bwd_w2", "L1_cond_ff_w1", "L1_cond_ff_w2")]),
        "cols": np.concatenate([columns(v) for v in (
            *[b[0:2 * D] for b in ada_b], a["L0_cond_g1"], a["L0_cond_be1"], a["L0_cond_g2"], a["L0_cond_be2"],
            a["L0_cond_bqkv"][0:2 * D], a["L0_cond_b1"], a["L1_cond_ssm_b1"], a["L1_cond_bwd_b1"],
            a["L1_cond_ff_b1"], a["L0_cond_bqkv"][2 * D:3 * D])], axis=1),
        "rows": np.stack([*[b[2 * D:3 * D] for b in ada_b], a["L0_cond_bproj"], a["L0_cond_b2"], a["L1_cond_ssm_b2"],
                          a["L1_cond_ff_b2"], a["L1_cond_bwd_b2"]]),
    }
    arrays = {k: np.ascontiguousarray(v) for k, v in arrays.items()}

    nc = bacc.Bacc("TRN2", target_bir_lowering=False, num_devices=1)
    dram = {k: nc.dram_tensor("in_" + k, v.shape, mybir.dt.from_np(v.dtype), kind="ExternalInput").ap() for k, v in arrays.items()}
    out = nc.dram_tensor("out", (NB, L, D), F32, kind="ExternalOutput").ap()
    rows = "b (u g p) n -> (b u) p g n"
    dram["x"] = dram["x"].rearrange(rows, u=NT, g=TG)
    dram["out"] = out.rearrange(rows, u=NT, g=TG)
    dram["x1"] = nc.dram_tensor("x1_dram", ((NB + 2) * NT, P, TG, D), F32, kind="Internal").ap()
    dram["gates"] = nc.dram_tensor("gates_dram", (4, NB + 1, 2, D), F32, kind="Internal").ap()
    build(nc, dram)
    r = run(nc, [{"in_" + k: v for k, v in arrays.items()}], core_ids=[0])
    return r.results[0]["out"]
```
